# Optimizing a Trainium2 kernel written in Bass

```python
import numpy as np
import jax
import jax.numpy as jnp

def _softmax(x, axis=-1):
    return jax.nn.softmax(x, axis=axis)

def _gelu(x):
    return jax.nn.gelu(x, approximate=True)

def _silu(x):
    return jax.nn.silu(x)

def _sigmoid(x):
    return jax.nn.sigmoid(x)

def _layernorm(x, axis=-1, eps=1e-05):
    m = jnp.mean(x, axis=axis, keepdims=True)
    v = jnp.var(x, axis=axis, keepdims=True)
    return (x - m) / jnp.sqrt(v + eps)

def _scatter_add(tgt, idx, src, axis=0):
    return tgt.at[idx].add(src)

def _segment_sum(src, seg, n):
    return jax.ops.segment_sum(src, seg, n)
kernel_name = 'mk_sandwich_d1_jaxref_r8_ccd3b9'

def setup_inputs(seed: int=0):
    np.random.seed(seed)
    _w = jnp.asarray

    def _L0_attn_setup():
        import jax, jax.numpy as jnp
        import numpy as np
        N_HEADS = 16
        SCALE = 8.0
        key = jax.random.key(seed)
        k1, k2, k3, k4 = jax.random.split(key, 4)
        b, n, d_model, inner = (8, 256, 128, 128)
        x = jax.random.normal(k1, (b, n, d_model), dtype=jnp.float32)
        Wqkv = jax.random.normal(k2, (3 * inner, d_model), dtype=jnp.float32) * (1.0 / np.sqrt(d_model))
        Wproj = jax.random.normal(k3, (d_model, inner), dtype=jnp.float32) * (1.0 / np.sqrt(inner))
        bproj = jax.random.normal(k4, (d_model,), dtype=jnp.float32) * 0.01
        return {'x': x, 'Wqkv': Wqkv, 'Wproj': Wproj, 'bproj': bproj}
    _L0_attn_in = _L0_attn_setup()

    def _L0_ffn_setup():
        import jax, jax.numpy as jnp
        import numpy as np
        DIM = 128
        DEPTH = 6
        HEADS = 16
        DIM_HEAD = 64
        WINDOW = 32
        INNER = HEADS * DIM_HEAD
        DIM_INNER = int(DIM * 4 * 2 / 3)
        QK_SCALE = 8.0

        def shift_tokens(t):
            a, s = jnp.split(t, 2, -1)
            s = jnp.pad(s, ((0, 0), (1, 0), (0, 0)))[:, :-1]
            return jnp.concatenate([a, s], -1)

        def l2norm(t):
            return t / jnp.maximum(jnp.linalg.norm(t, axis=-1, keepdims=True), 1e-12)

        def rotate_half(x):
            x1, x2 = jnp.split(x, 2, -1)
            return jnp.concatenate([-x2, x1], -1)

        def rotary_tables(n):
            half = jnp.arange(0, DIM_HEAD, 2, dtype=jnp.float32)
            inv_freq = 1.0 / 10000.0 ** (half / DIM_HEAD)
            t = jnp.arange(n, dtype=jnp.float32)
            freqs = t[:, None] * inv_freq[None, :]
            freqs = jnp.concatenate([freqs, freqs], -1)
            base_scale = (half + 0.4 * DIM_HEAD) / (1.4 * DIM_HEAD)
            power = (t - n // 2) / (WINDOW // 2)
            scale = base_scale[None, :] ** power[:, None]
            scale = jnp.concatenate([scale, scale], -1)
            return (freqs, scale)

        def local_attention(q, k, v):
            b, h, n, d = q.shape
            w = WINDOW
            nw = n // w
            bq = q.reshape(b, h, nw, w, d)
            bk = k.reshape(b, h, nw, w, d)
            bv = v.reshape(b, h, nw, w, d)

            def look(t):
                p = jnp.pad(t, ((0, 0), (0, 0), (1, 0), (0, 0), (0, 0)))
                return jnp.concatenate([p[:, :, :nw], p[:, :, 1:]], axis=3)
            bk2, bv2 = (look(bk), look(bv))
            seq = jnp.arange(n).reshape(nw, w)
            seq_p = jnp.pad(seq, ((1, 0), (0, 0)), constant_values=-1)
            jt = jnp.concatenate([seq_p[:nw], seq_p[1:]], axis=1)
            it = seq[:, :, None]
            jb = jt[:, None, :]
            mask = (it < jb) | (it > jb + w) | (jb == -1)
            sim = jnp.einsum('bhwie,bhwje->bhwij', bq, bk2) * QK_SCALE
            sim = jnp.where(mask, -jnp.finfo(sim.dtype).max, sim)
            attn = jax.nn.softmax(sim, -1)
            out = jnp.einsum('bhwij,bhwje->bhwie', attn, bv2)
            return out.reshape(b, h, n, d)

        def attn_layer(x, Wqkv, qs, ksc, Wo):
            b, n, _ = x.shape
            qkv = x @ Wqkv
            q, k, v = jnp.split(qkv, 3, -1)
            sh = lambda t: t.reshape(b, n, HEADS, DIM_HEAD).transpose(0, 2, 1, 3)
            q, k, v = (sh(q), sh(k), sh(v))
            q = l2norm(q) * qs
            k = l2norm(k) * ksc
            freqs, scale = rotary_tables(n)
            cos, sin = (jnp.cos(freqs), jnp.sin(freqs))
            q = q * cos * scale + rotate_half(q) * sin * scale
            inv = 1.0 / scale
            k = k * cos * inv + rotate_half(k) * sin * inv
            out = local_attention(q, k, v)
            out = out.transpose(0, 2, 1, 3).reshape(b, n, INNER)
            return out @ Wo

        def ffn_layer(x, g, bln, W1, b1, W2, b2):
            mu = x.mean(-1, keepdims=True)
            var = ((x - mu) ** 2).mean(-1, keepdims=True)
            xn = (x - mu) / jnp.sqrt(var + 1e-05) * g + bln
            hg = xn @ W1 + b1
            a, gate = jnp.split(hg, 2, -1)
            return a * jax.nn.gelu(gate, approximate=False) @ W2 + b2
        key = jax.random.key(seed)
        ks = jax.random.split(key, 8)
        B, N = (2, 256)
        init = lambda k, shape: jax.random.normal(k, shape, jnp.float32) * 0.02
        return {'x': jax.random.normal(ks[0], (B, N, DIM), jnp.float32), 'Wqkv': init(ks[1], (DEPTH, DIM, 3 * INNER)), 'q_scale': jnp.ones((DEPTH, DIM_HEAD), jnp.float32), 'k_scale': jnp.ones((DEPTH, DIM_HEAD), jnp.float32), 'Wo': init(ks[2], (DEPTH, INNER, DIM)), 'ln_g': jnp.ones((DEPTH, DIM), jnp.float32), 'ln_b': jnp.zeros((DEPTH, DIM), jnp.float32), 'W1': init(ks[3], (DEPTH, DIM, 2 * DIM_INNER)), 'b1': jnp.zeros((DEPTH, 2 * DIM_INNER), jnp.float32), 'W2': init(ks[4], (DEPTH, DIM_INNER, DIM)), 'b2': jnp.zeros((DEPTH, DIM), jnp.float32)}
    _L0_ffn_in = _L0_ffn_setup()
    _d = {'L0_attn_x': _L0_attn_in['x'], 'L0_attn_Wqkv': _L0_attn_in['Wqkv'], 'L0_attn_Wproj': _L0_attn_in['Wproj'], 'L0_attn_bproj': _L0_attn_in['bproj'], 'L0_ffn_Wqkv': _L0_ffn_in['Wqkv'], 'L0_ffn_q_scale': _L0_ffn_in['q_scale'], 'L0_ffn_k_scale': _L0_ffn_in['k_scale'], 'L0_ffn_Wo': _L0_ffn_in['Wo'], 'L0_ffn_ln_g': _L0_ffn_in['ln_g'], 'L0_ffn_ln_b': _L0_ffn_in['ln_b'], 'L0_ffn_W1': _L0_ffn_in['W1'], 'L0_ffn_b1': _L0_ffn_in['b1'], 'L0_ffn_W2': _L0_ffn_in['W2'], 'L0_ffn_b2': _L0_ffn_in['b2']}
    _x0 = _d['L0_attn_x']
    _d['L0_attn_x'] = jax.random.normal(jax.random.fold_in(jax.random.key(seed), 1), (2, 1024, 128), dtype=_x0.dtype)
    del _x0
    return _d

def reference(L0_attn_x, L0_attn_Wqkv, L0_attn_Wproj, L0_attn_bproj, L0_ffn_Wqkv, L0_ffn_q_scale, L0_ffn_k_scale, L0_ffn_Wo, L0_ffn_ln_g, L0_ffn_ln_b, L0_ffn_W1, L0_ffn_b1, L0_ffn_W2, L0_ffn_b2):

    def _L0_attn_ref(x, Wqkv, Wproj, bproj):
        import jax, jax.numpy as jnp
        import numpy as np
        N_HEADS = 16
        SCALE = 8.0
        b, n, _ = x.shape
        qkv = jnp.einsum('bnm,fm->bnf', x, Wqkv)
        qkv = qkv.reshape(b, n, N_HEADS, -1)
        dh = qkv.shape[3] // 3
        q, k, v = (qkv[..., :dh], qkv[..., dh:2 * dh], qkv[..., 2 * dh:])
        scores = jnp.einsum('bnhd,bngd->bnhg', q, k) / SCALE
        attn = jax.nn.softmax(scores, axis=-1)
        out = jnp.einsum('bnhg,bngd->bnhd', attn, v)
        out = out.reshape(b, n, -1)
        return jnp.einsum('bni,mi->bnm', out, Wproj) + bproj

    def _L0_ffn_ref(x, Wqkv, q_scale, k_scale, Wo, ln_g, ln_b, W1, b1, W2, b2):
        import jax, jax.numpy as jnp
        import numpy as np
        DIM = 128
        DEPTH = 6
        HEADS = 16
        DIM_HEAD = 64
        WINDOW = 32
        INNER = HEADS * DIM_HEAD
        DIM_INNER = int(DIM * 4 * 2 / 3)
        QK_SCALE = 8.0

        def shift_tokens(t):
            a, s = jnp.split(t, 2, -1)
            s = jnp.pad(s, ((0, 0), (1, 0), (0, 0)))[:, :-1]
            return jnp.concatenate([a, s], -1)

        def l2norm(t):
            return t / jnp.maximum(jnp.linalg.norm(t, axis=-1, keepdims=True), 1e-12)

        def rotate_half(x):
            x1, x2 = jnp.split(x, 2, -1)
            return jnp.concatenate([-x2, x1], -1)

        def rotary_tables(n):
            half = jnp.arange(0, DIM_HEAD, 2, dtype=jnp.float32)
            inv_freq = 1.0 / 10000.0 ** (half / DIM_HEAD)
            t = jnp.arange(n, dtype=jnp.float32)
            freqs = t[:, None] * inv_freq[None, :]
            freqs = jnp.concatenate([freqs, freqs], -1)
            base_scale = (half + 0.4 * DIM_HEAD) / (1.4 * DIM_HEAD)
            power = (t - n // 2) / (WINDOW // 2)
            scale = base_scale[None, :] ** power[:, None]
            scale = jnp.concatenate([scale, scale], -1)
            return (freqs, scale)

        def local_attention(q, k, v):
            b, h, n, d = q.shape
            w = WINDOW
            nw = n // w
            bq = q.reshape(b, h, nw, w, d)
            bk = k.reshape(b, h, nw, w, d)
            bv = v.reshape(b, h, nw, w, d)

            def look(t):
                p = jnp.pad(t, ((0, 0), (0, 0), (1, 0), (0, 0), (0, 0)))
                return jnp.concatenate([p[:, :, :nw], p[:, :, 1:]], axis=3)
            bk2, bv2 = (look(bk), look(bv))
            seq = jnp.arange(n).reshape(nw, w)
            seq_p = jnp.pad(seq, ((1, 0), (0, 0)), constant_values=-1)
            jt = jnp.concatenate([seq_p[:nw], seq_p[1:]], axis=1)
            it = seq[:, :, None]
            jb = jt[:, None, :]
            mask = (it < jb) | (it > jb + w) | (jb == -1)
            sim = jnp.einsum('bhwie,bhwje->bhwij', bq, bk2) * QK_SCALE
            sim = jnp.where(mask, -jnp.finfo(sim.dtype).max, sim)
            attn = jax.nn.softmax(sim, -1)
            out = jnp.einsum('bhwij,bhwje->bhwie', attn, bv2)
            return out.reshape(b, h, n, d)

        def attn_layer(x, Wqkv, qs, ksc, Wo):
            b, n, _ = x.shape
            qkv = x @ Wqkv
            q, k, v = jnp.split(qkv, 3, -1)
            sh = lambda t: t.reshape(b, n, HEADS, DIM_HEAD).transpose(0, 2, 1, 3)
            q, k, v = (sh(q), sh(k), sh(v))
            q = l2norm(q) * qs
            k = l2norm(k) * ksc
            freqs, scale = rotary_tables(n)
            cos, sin = (jnp.cos(freqs), jnp.sin(freqs))
            q = q * cos * scale + rotate_half(q) * sin * scale
            inv = 1.0 / scale
            k = k * cos * inv + rotate_half(k) * sin * inv
            out = local_attention(q, k, v)
            out = out.transpose(0, 2, 1, 3).reshape(b, n, INNER)
            return out @ Wo

        def ffn_layer(x, g, bln, W1, b1, W2, b2):
            mu = x.mean(-1, keepdims=True)
            var = ((x - mu) ** 2).mean(-1, keepdims=True)
            xn = (x - mu) / jnp.sqrt(var + 1e-05) * g + bln
            hg = xn @ W1 + b1
            a, gate = jnp.split(hg, 2, -1)
            return a * jax.nn.gelu(gate, approximate=False) @ W2 + b2
        for i in range(DEPTH):
            x = attn_layer(shift_tokens(x), Wqkv[i], q_scale[i], k_scale[i], Wo[i]) + x
            x = ffn_layer(shift_tokens(x), ln_g[i], ln_b[i], W1[i], b1[i], W2[i], b2[i]) + x
        return x
    x = L0_attn_x
    x = x + _layernorm(_L0_attn_ref(_layernorm(x, axis=-1), L0_attn_Wqkv, L0_attn_Wproj, L0_attn_bproj), axis=-1)
    x = x + _layernorm(_L0_ffn_ref(_layernorm(x, axis=-1), L0_ffn_Wqkv, L0_ffn_q_scale, L0_ffn_k_scale, L0_ffn_Wo, L0_ffn_ln_g, L0_ffn_ln_b, L0_ffn_W1, L0_ffn_b1, L0_ffn_W2, L0_ffn_b2), axis=-1)
    return x

_drawn_inputs = setup_inputs


def setup_inputs(seed=0):
    import zlib

    import numpy as np

    out = dict(_drawn_inputs(seed))
    spreads = {'L0_ffn_q_scale': (1.0, 0.6),
     'L0_ffn_k_scale': (1.0, 0.6),
     'L0_ffn_ln_g': (1.0, 0.6),
     'L0_ffn_ln_b': (0.0, 0.8),
     'L0_ffn_b1': (0.0, 0.8),
     'L0_ffn_b2': (0.0, 0.328)}
    factors = {'L0_ffn_W1': 4.504, 'L0_ffn_W2': 4.443}
    for name, (base, spread) in spreads.items():
        noise = np.random.default_rng([zlib.crc32(name.encode()), seed]).standard_normal(out[name].shape)
        drawn = base * np.exp(spread * noise) if base else spread * noise
        out[name] = jnp.asarray(drawn.astype(out[name].dtype))
    for name, factor in factors.items():
        out[name] = (out[name] * factor).astype(out[name].dtype)
    return out
```

```python
from contextlib import ExitStack

import concourse.bass as bass
from concourse import mybir

F32 = mybir.dt.float32
BF16 = mybir.dt.bfloat16
I32 = mybir.dt.int32
ALU = mybir.AluOpType
ACT = mybir.ActivationFunctionType
AX = mybir.AxisListType

P = 128
B, N, D = 2, 1024, 128
T = B * N
GT = 512
NG = T // GT
NT = T // P
EPS = 1e-5

H1, D1 = 16, 8
QT = N // P

DEPTH, HEADS, DH, WIN = 6, 16, 64, 32
INNER = HEADS * DH
NC = INNER // P
F = 341
FCH = [(0, 128), (128, 128), (256, F - 256)]
NEG = -1e30
RSQRT_MAGIC = 0x5F3759DF
TPG = GT // P
WPT = P // WIN
XPAD = WIN
XB = XPAD + N + 1


def xcol(t0):
    return (t0 // N) * XB + XPAD + t0 % N


def layer_norm_pe(nc, pe, ones_d, src, sq, ps_mean, ps_var, src_ready, sq_ready, mean_ready, var_ready):
    for g in range(NG):
        pe.wait_ge(src_ready, g + 1)
        nc.tensor.matmul(ps_mean(g), ones_d[:], src(g), start=True, stop=True).then_inc(mean_ready, 1)
    for g in range(NG):
        pe.wait_ge(sq_ready, g + 1)
        nc.tensor.matmul(ps_var(g), ones_d[:], sq(g), start=True, stop=True).then_inc(var_ready, 1)


def layer_norm_act(nc, act, eps, xc, sq, ps_var, sd, xc_ready, sq_ready, var_ready, sd_ready):
    for g in range(NG):
        act.wait_ge(xc_ready, g + 1)
        nc.scalar.activation(sq(g), xc(g), ACT.Square).then_inc(sq_ready, 1)
    for g in range(NG):
        act.wait_ge(var_ready, g + 1)
        nc.scalar.activation(sd(g), ps_var(g), ACT.Sqrt, bias=eps[:, 0:1]).then_inc(sd_ready, 1)


def layer_norm_dve(nc, dve, src, xc, ps_mean, sd, out, mean_ready, xc_ready, sd_ready, rs_ready, ln_ready):
    for g in range(NG):
        dve.wait_ge(mean_ready, g + 1)
        nc.vector.tensor_tensor(xc(g), src(g), ps_mean(g), ALU.subtract).then_inc(xc_ready, 1)
    for g in range(NG):
        dve.wait_ge(sd_ready, g + 1)
        nc.vector.reciprocal(sd(g), sd(g)).then_inc(rs_ready, 1)
        dve.wait_ge(rs_ready, g + 1)
        nc.vector.tensor_tensor(out(g), xc(g), sd(g), ALU.mult).then_inc(ln_ready, 1)


def grp(t):
    return lambda g: t[:, g * GT:(g + 1) * GT]


def load_and_project(nc, c, x, wqkv):
    HV = 10
    QKV = 3 * H1 * D1
    with ExitStack() as ctx:
        sb = lambda n, s, d=F32: ctx.enter_context(nc.sbuf_tensor(n, s, d))
        sem = lambda n: ctx.enter_context(nc.semaphore(n))
        ps = ctx.enter_context(nc.psum_tensor("prep_ps", [P, 8, GT], F32))
        xin = sb("xin", [P, NT, D])
        win = sb("win", [P, 3, D])
        wT = sb("wT", [P, QKV])
        xc, sq, sd, xn = (sb(n, [P, T]) for n in ("xc", "sq", "sd", "xn"))
        qkv = sb("qkv", [P, 4, H1, 3, D1])
        qk_prod = sb("qk_prod", [P, 2, H1, H1, D1])
        pv_prod = sb("pv_prod", [P, 2, H1, D1, H1])
        prob = sb("prob", [P, 2, H1, H1])
        nmax, den = sb("nmax", [P, H1]), sb("den", [P, H1])
        num = sb("num", [P, H1, D1])
        x_loaded, w_loaded, const_loaded = sem("x_loaded"), sem("w_loaded"), sem("p_const_loaded")
        eps_ready, xT_filled, wT_filled, x0_ready = sem("eps_ready"), sem("xT_filled"), sem("wT_filled"), sem("x0_ready")
        wT_ready = sem("wT_ready")
        mean_ready, xc_ready, sq_ready, var_ready = sem("mean_ready"), sem("xc_ready"), sem("sq_ready"), sem("var_ready")
        sd_ready, rs_ready, ln_ready = sem("sd_ready"), sem("rs_ready"), sem("ln_ready")
        qkv_filled, qkv_ready, qk_multiplied, scored = sem("qkv_filled"), sem("qkv_ready"), sem("qk_multiplied"), sem("scored")
        maxed, centred, exped, pv_pool, pv_dve = sem("maxed"), sem("centred"), sem("exped"), sem("pv_pool"), sem("pv_dve")
        den_step, pv_summed, o_ready = sem("den_step"), sem("pv_summed"), sem("o_ready")
        psf = ps[:].rearrange("p a b -> p (a b)")
        x_rows = x.rearrange("b (t p) d -> p (b t) d", p=P)

        def loop(eng, body):
            body(0, 0)
            with eng.Fori(0, 3) as i:
                for u in range(4):
                    body(i * 4 + (u + 1), u + 1)
            for t in range(13, NT + 1):
                body(t, t)

        with nc.Block() as block:

            @block.sync
            def _(sp):
                for h in range(2):
                    sp.dma_start(xin[:, 8 * h:8 * h + 8, :], x_rows[:, 8 * h:8 * h + 8, :]).then_inc(x_loaded, 16)
                sp.dma_start(c.rope[:], c.rope_dram).then_inc(const_loaded, 16)
                sp.wait_ge(const_loaded, 16)

            @block.gpsimd
            def _(pool):
                nc.gpsimd.memset(c.ones_d[:], 1.0 / D).then_inc(eps_ready, 1)
                nc.gpsimd.memset(c.eps[:], EPS).then_inc(eps_ready, 1)
                nc.gpsimd.memset(c.xsA[:], 0.0).then_inc(eps_ready, 1)
                nc.gpsimd.memset(c.xsF[:], 0.0).then_inc(eps_ready, 1)
                pool.wait_ge(eps_ready, 4)
                pool.sem_inc(pv_pool, 4)

                def body(t, k):
                    if k < NT:
                        pool.wait_ge(qkv_ready, t + 1)
                        pool.wait_ge(scored, t + 1)
                        q, kk = qkv[:, k % 4, :, 0, :], qkv[:, k % 4, :, 1, :]
                        nc.gpsimd.tensor_tensor(qk_prod[:, k % 2, :, :, :], q[:, :, None, :].broadcast_to([P, H1, H1, D1]),
                                                kk[:, None, :, :].broadcast_to([P, H1, H1, D1]), ALU.mult).then_inc(qk_multiplied, 1)
                    if k >= 1:
                        pool.wait_ge(exped, t)
                        pool.wait_ge(pv_summed, t)
                        v = qkv[:, (k - 1) % 4, :, 2, :].rearrange("p g d -> p d g")
                        nc.gpsimd.tensor_tensor(pv_prod[:, (k - 1) % 2, 0:HV, :, :],
                                                prob[:, (k - 1) % 2, 0:HV, None, :].broadcast_to([P, HV, D1, H1]),
                                                v[:, None, :, :].broadcast_to([P, HV, D1, H1]), ALU.mult).then_inc(pv_pool, 1)

                loop(pool, body)

            @block.scalar
            def _(act):
                act.dma_start(c.ident[:], c.ident_dram).then_inc(w_loaded, 16)
                act.dma_start(win[:], wqkv.rearrange("(a p) m -> p a m", p=P)).then_inc(w_loaded, 16)
                act.dma_start(c.mask32[:], c.mask_dram).then_inc(w_loaded, 16)
                act.wait_ge(wT_filled, 1)
                nc.scalar.activation(wT[:], psf[:, 4 * GT:4 * GT + QKV], ACT.Copy).then_inc(wT_ready, 1)
                act.wait_ge(eps_ready, 4)
                layer_norm_act(nc, act, c.eps, grp(xc), grp(sq), lambda g: ps[:, 4 + g, :], grp(sd),
                               xc_ready, sq_ready, var_ready, sd_ready)

                def body(t, k):
                    if k < NT:
                        act.wait_ge(qkv_filled, t + 1)
                        act.wait_ge(pv_pool, t + 1)
                        act.wait_ge(pv_dve, t + 1)
                        nc.scalar.activation(qkv[:, k % 4, :, :, :].rearrange("p h c d -> p (h c d)"), ps[:, k % 2, 0:QKV],
                                             ACT.Copy).then_inc(qkv_ready, 1)
                    if k >= 1:
                        act.wait_ge(centred, t)
                        nc.scalar.activation(prob[:, (k - 1) % 2, :, :], prob[:, (k - 1) % 2, :, :], ACT.Exp,
                                             scale=1.0 / 8.0).then_inc(exped, 1)

                loop(act, body)

            @block.vector
            def _(dve):
                for g in range(NG):
                    dve.wait_ge(xT_filled, g + 1)
                    nc.vector.tensor_copy(c.x0[:, g * GT:(g + 1) * GT], ps[:, g, :]).then_inc(x0_ready, 1)
                dve.wait_ge(w_loaded, 48)
                nc.vector.tensor_copy(c.identb[:], c.ident[:]).then_inc(x0_ready, 1)
                nc.vector.tensor_copy(c.mask[:], c.mask32[:]).then_inc(x0_ready, 1)
                dve.wait_ge(x0_ready, NG + 2)
                layer_norm_dve(nc, dve, grp(c.x0), grp(xc), lambda g: ps[:, g, :], grp(sd), grp(xn),
                               mean_ready, xc_ready, sd_ready, rs_ready, ln_ready)
                dve.sem_inc(scored, 2)
                dve.sem_inc(pv_summed, 2)
                dve.sem_inc(pv_dve, 4)
                dve.sem_inc(o_ready, 1)

                def body(t, k):
                    if k < NT:
                        pr = prob[:, k % 2, :, :]
                        dve.wait_ge(qk_multiplied, t + 1)
                        dve.wait_ge(pv_pool, t + 3)
                        nc.vector.tensor_reduce(pr, qk_prod[:, k % 2, :, :, :], AX.X, ALU.add).then_inc(scored, 1)
                        dve.wait_ge(scored, t + 3)
                        nc.vector.tensor_reduce(nmax[:], pr, AX.X, ALU.max, negate=True).then_inc(maxed, 1)
                        dve.wait_ge(maxed, t + 1)
                        nc.vector.tensor_tensor(pr, pr, nmax[:, :, None].broadcast_to([P, H1, H1]), ALU.add).then_inc(centred, 1)
                    if k >= 1:
                        pr = prob[:, (k - 1) % 2, :, :]
                        v = qkv[:, (k - 1) % 4, :, 2, :].rearrange("p g d -> p d g")
                        dve.wait_ge(exped, t)
                        nc.vector.tensor_tensor(pv_prod[:, (k - 1) % 2, HV:, :, :],
                                                pr[:, HV:, None, :].broadcast_to([P, H1 - HV, D1, H1]),
                                                v[:, None, :, :].broadcast_to([P, H1 - HV, D1, H1]), ALU.mult).then_inc(pv_dve, 1)
                        dve.wait_ge(o_ready, t)
                        nc.vector.tensor_reduce(den[:], pr, AX.X, ALU.add).then_inc(den_step, 1)
                        dve.wait_ge(pv_pool, t + 4)
                        dve.wait_ge(pv_dve, t + 4)
                        nc.vector.tensor_reduce(num[:], pv_prod[:, (k - 1) % 2, :, :, :], AX.X, ALU.add).then_inc(pv_summed, 1)
                        dve.wait_ge(den_step, 2 * t - 1)
                        nc.vector.reciprocal(den[:], den[:]).then_inc(den_step, 1)
                        dve.wait_ge(pv_summed, t + 2)
                        dve.wait_ge(den_step, 2 * t)
                        nc.vector.tensor_tensor(c.o_tok[:, bass.ds(t - 1, 1), :].rearrange("p o (h d) -> p (o h) d", h=H1), num[:],
                                                den[:, :, None].broadcast_to([P, H1, D1]), ALU.mult).then_inc(o_ready, 1)

                loop(dve, body)

            @block.tensor
            def _(pe):
                pe.wait_ge(w_loaded, 48)
                pe.wait_ge(x_loaded, 32)
                for a in range(3):
                    m = nc.tensor.transpose(ps[:, 4, a * P:(a + 1) * P], win[:, a, :], c.ident[:])
                m.then_inc(wT_filled, 1)
                for g in range(NG):
                    for j in range(TPG):
                        m = nc.tensor.transpose(ps[:, g, j * P:(j + 1) * P], xin[:, g * TPG + j, :], c.ident[:])
                    m.then_inc(xT_filled, 1)
                pe.wait_ge(eps_ready, 4)
                pe.wait_ge(x0_ready, NG)
                pe.wait_ge(wT_ready, 1)
                layer_norm_pe(nc, pe, c.ones_d, grp(c.x0), grp(sq), lambda g: ps[:, g, :],
                              lambda g: ps[:, 4 + g, :], x0_ready, sq_ready, mean_ready, var_ready)
                for t in range(NT):
                    pe.wait_ge(ln_ready, t // TPG + 1)
                    if t >= 2:
                        pe.wait_ge(qkv_ready, t - 1)
                    nc.tensor.matmul(ps[:, t % 2, 0:QKV], xn[:, t * P:(t + 1) * P], wT[:], start=True, stop=True).then_inc(qkv_filled, 1)


def shift_copy(nc, src, dst, g):
    col = xcol(g * GT)
    nc.vector.tensor_copy(dst[0:64, col:col + GT], src[0:64, g * GT:(g + 1) * GT])
    return nc.vector.tensor_copy(dst[64:P, col + 1:col + 1 + GT], src[64:P, g * GT:(g + 1) * GT])


def project(nc, c, wproj, bproj, weights):
    with ExitStack() as ctx:
        sb = lambda n, s, d=F32: ctx.enter_context(nc.sbuf_tensor(n, s, d))
        sem = lambda n: ctx.enter_context(nc.semaphore(n))
        ps = ctx.enter_context(nc.psum_tensor("proj_ps", [P, 8, GT], F32))
        w_in, wT, bp = sb("wp_in", [P, P]), sb("wpT", [P, P]), sb("bp", [P, 1])
        oT, a, xc, sq, sd, y = (sb(n, [P, T]) for n in ("oT", "attn", "c_xc", "c_sq", "c_sd", "c_y"))
        wp_loaded, oT_filled, oT_ready, wpT_filled, wpT_ready = (sem(n) for n in (
            "wp_loaded", "oT_filled", "oT_ready", "wpT_filled", "wpT_ready"))
        proj_filled, attn_ready, x1_ready, xT_shifted = sem("proj_filled"), sem("attn_ready"), sem("x1_ready"), sem("xT_shifted")
        ln = [[sem(f"c{r}_{n}") for n in ("mean", "xc", "sq", "var", "sd", "rs", "ln")] for r in range(2)]
        ps_mean, ps_var = lambda g: ps[:, g, :], lambda g: ps[:, 4 + g, :]
        with nc.Block() as block:

            @block.sync
            def _(sp):
                sp.dma_start(w_in[:], wproj).then_inc(wp_loaded, 16)
                sp.dma_start(bp[:], bproj.rearrange("(p o) -> p o", o=1)).then_inc(wp_loaded, 16)
                weights.load_qkv(sp, 0)
                weights.load_wo(sp, 0)
                weights.load_ffn(sp, 0)

            @block.tensor
            def _(pe):
                pe.wait_ge(wp_loaded, 32)
                nc.tensor.transpose(ps[:, 4, 0:P], w_in[:], c.ident[:]).then_inc(wpT_filled, 1)
                for g in range(NG):
                    for j in range(TPG):
                        m = nc.tensor.transpose(ps[:, g, j * P:(j + 1) * P], c.o_tok[:, g * TPG + j, :], c.ident[:])
                    m.then_inc(oT_filled, 1)
                pe.wait_ge(wpT_ready, 1)
                for g in range(NG):
                    pe.wait_ge(oT_ready, g + 1)
                    nc.tensor.matmul(ps[:, 4 + g, :], wT[:], oT[:, g * GT:(g + 1) * GT], start=True, stop=True).then_inc(proj_filled, 1)
                mean, xcr, sqr, var, sdr, rs, done = ln[0]
                pe.wait_ge(attn_ready, NG)
                layer_norm_pe(nc, pe, c.ones_d, grp(a), grp(sq), ps_mean, ps_var, attn_ready, sqr, mean, var)
                mean, xcr, sqr, var, sdr, rs, done = ln[1]
                layer_norm_pe(nc, pe, c.ones_d, grp(c.x1), grp(sq), ps_mean, ps_var, x1_ready, sqr, mean, var)

            @block.scalar
            def _(act):
                act.wait_ge(wpT_filled, 1)
                nc.scalar.activation(wT[:], ps[:, 4, 0:P], ACT.Copy).then_inc(wpT_ready, 1)
                for g in range(NG):
                    act.wait_ge(oT_filled, g + 1)
                    nc.scalar.activation(oT[:, g * GT:(g + 1) * GT], ps[:, g, :], ACT.Copy).then_inc(oT_ready, 1)
                for r in range(2):
                    mean, xcr, sqr, var, sdr, rs, done = ln[r]
                    layer_norm_act(nc, act, c.eps, grp(xc), grp(sq), ps_var, grp(sd), xcr, sqr, var, sdr)

            @block.vector
            def _(dve):
                dve.wait_ge(wp_loaded, 32)
                for g in range(NG):
                    dve.wait_ge(proj_filled, g + 1)
                    nc.vector.tensor_scalar(a[:, g * GT:(g + 1) * GT], ps[:, 4 + g, :], bp[:, 0:1], None, ALU.add).then_inc(attn_ready, 1)
                dve.wait_ge(attn_ready, NG)
                mean, xcr, sqr, var, sdr, rs, done = ln[0]
                layer_norm_dve(nc, dve, grp(a), grp(xc), ps_mean, grp(sd), grp(y), mean, xcr, sdr, rs, done)
                for g in range(NG):
                    dve.wait_ge(done, g + 1)
                    nc.vector.tensor_tensor(grp(c.x1)(g), grp(c.x1)(g), grp(y)(g), ALU.add).then_inc(x1_ready, 1)
                dve.wait_ge(x1_ready, NG)
                mean, xcr, sqr, var, sdr, rs, done = ln[1]
                layer_norm_dve(nc, dve, grp(c.x1), grp(xc), ps_mean, grp(sd), grp(c.xT), mean, xcr, sdr, rs, done)
                for g in range(NG):
                    dve.wait_ge(done, g + 1)
                    shift_copy(nc, c.xT, c.xsA, g).then_inc(xT_shifted, 1)
                dve.wait_ge(xT_shifted, NG)


class Weights:
    QKV, WO, FFN = 16 * 4, 16, 16 * 13

    def __init__(self, nc, ctx, wqkv, qs, ks, wo, lg, lb, w1, b1, w2, b2):
        sb = lambda n, s, d=F32: ctx.enter_context(nc.sbuf_tensor(n, s, d))
        self.dram = (wqkv, qs, ks, wo, lg, lb, w1, b1, w2, b2)
        self.qkv, self.wo = sb("w_qkv", [P, 3 * INNER]), sb("w_o", [P, NC, D])
        self.scales = sb("qk_scales", [P, 2, DH])
        self.lg, self.lb, self.b2 = sb("ln_g", [P, 1]), sb("ln_b", [P, 1]), sb("b2", [P, 1])
        self.w1, self.b1, self.w2 = sb("w1", [P, 2 * F]), sb("b1", [P, 2, len(FCH)]), sb("w2", [P, len(FCH), D])
        self.qkv_loaded, self.wo_loaded, self.ffn_loaded = (
            ctx.enter_context(nc.semaphore(n)) for n in ("w_qkv_loaded", "w_o_loaded", "w_ffn_loaded"))

    def load_qkv(self, eng, layer):
        wqkv, qs, ks = self.dram[0:3]
        for h in range(2):
            cols = slice(h * 3 * INNER // 2, (h + 1) * 3 * INNER // 2)
            eng.dma_start(self.qkv[:, cols], wqkv[bass.ds(layer, 1), :, cols].rearrange("o d f -> (o d) f")).then_inc(self.qkv_loaded, 16)
        for i, t in enumerate((qs, ks)):
            eng.dma_start(self.scales[:, i, :], t[bass.ds(layer, 1), :].broadcast_to([P, DH])).then_inc(self.qkv_loaded, 16)

    def load_wo(self, eng, layer):
        wo = self.dram[3]
        eng.dma_start(self.wo[:], wo[bass.ds(layer, 1), :, :].rearrange("o (c p) m -> (o p) c m", p=P)).then_inc(self.wo_loaded, 16)

    def load_ffn(self, eng, layer):
        lg, lb, w1, b1, w2, b2 = self.dram[4:]
        one, loaded = bass.ds(layer, 1), self.ffn_loaded
        for dst, src in ((self.lg, lg), (self.lb, lb), (self.b2, b2)):
            eng.dma_start(dst[:], src[one, :].rearrange("o (p q) -> (o p) q", q=1)).then_inc(loaded, 16)
        eng.dma_start(self.w1[:], w1[one, :, :].rearrange("o d f -> (o d) f")).then_inc(loaded, 16)
        for part in range(2):
            for i, (off, sz) in enumerate(FCH):
                src = b1[one, part * F + off:part * F + off + sz].rearrange("o (p q) -> (o p) q", q=1)
                eng.dma_start(self.b1[0:sz, part, i:i + 1], src).then_inc(loaded, 16)
        for i, (off, sz) in enumerate(FCH):
            eng.dma_start(self.w2[0:sz, i, :], w2[one, off:off + sz, :].rearrange("o f m -> (o f) m")).then_inc(loaded, 16)


def layer_order():
    order = []

    def ffn(groups):
        for kind in ("mean", "var", "h0", "h1", "h2", "y"):
            order.extend((kind, g) for g in groups)

    for i in range(NT + 2):
        if 1 <= i <= NT:
            order.extend([("qT", i - 1), ("kT", i - 1)])
        if i >= 2:
            order.append(("OT", i - 2))
        if i < NT:
            order.extend([("q", i), ("k", i)])
        if i >= 2 and (i - 2) % TPG == TPG - 1:
            order.append(("W", (i - 2) // TPG))
        if 1 <= i <= NT:
            order.append(("S", i - 1))
        if i < NT:
            order.append(("v0", i))
        if 1 <= i <= NT:
            order.append(("PT", i - 1))
        if i < NT:
            order.append(("v1", i))
        if 1 <= i <= NT:
            order.append(("O", i - 1))
        if i == NT:
            ffn((0, 1))
    ffn((2, 3))
    return order


ORDER = layer_order()
PLACE = {unit: n for n, unit in enumerate(ORDER)}
HIDDEN = {unit: n for n, unit in enumerate(u for u in ORDER if u[0][0] == "h")}
KINDS = ("q", "k", "v0", "v1", "qT", "kT", "S", "PT", "O", "OT", "W", "mean", "var", "h0", "h1", "h2", "y")
RING = 4


def layers(nc, c, wt):
    with ExitStack() as ctx:
        sb = lambda n, s, d=F32: ctx.enter_context(nc.sbuf_tensor(n, s, d))
        ring = ctx.enter_context(nc.psum_tensor("ring", [P, RING, 2 * GT], F32))
        raw = sb("raw", [P, 2, INNER])
        sqr = sb("squares", [P, 2, INNER])
        rot = sb("rot", [P, 2, INNER])
        rot2 = sb("rot2", [P, 2, INNER])
        ss, yv, tv, uv = (sb(n, [P, 2 * HEADS]) for n in ("ss", "rsqrt", "newton1", "newton2"))
        rope = sb("rope_layer", [P, 2, 2, QT, DH])
        qT, kT = sb("qT", [P, NC, P]), sb("kT", [P, NC, 2, WIN + P])
        v = sb("v_win", [P, 2, WPT, NC, DH])
        prob = sb("l_prob", [P, NC, 2, 2 * WIN])
        nm, rs, rr = sb("nmax_l", [P, 2, NC]), sb("rsum", [P, NC, 2]), sb("rrec", [P, NC, 2])
        pT, o = sb("pT", [P, NC, P]), sb("o_win", [P, NC, 2, DH])
        oT = sb("oT_grp", [P, NC, GT])
        xc, sq, sd, xn = (sb(n, [P, 2, GT]) for n in ("f_xc", "f_sq", "f_sd", "f_xn"))
        gl, hh = sb("gelu", [P, 2, GT]), sb("hidden", [P, 2, len(FCH), GT])
        kT_cleared = ctx.enter_context(nc.semaphore("kT_cleared"))
        sems = []

        def sem(n):
            sems.append(ctx.enter_context(nc.semaphore(n)))
            return sems[-1]

        filled = {kind: sem(f"{kind}_filled_l") for kind in KINDS}
        drained = [sem(f"slot{s}_drained") for s in range(RING)]
        rope_step, rope_ready = sem("rope_step"), sem("rope_ready")
        sq_ready, t1_ready, t2_ready, rot_ready, unit_ready = (
            [sem(f"{n}_{x}_ready") for x in "qk"] for n in ("sq", "t1", "t2", "rot", "unit"))
        ss_ready, rsqrt_step, rsqrt_ready = sem("ss_ready"), sem("rsqrt_step"), sem("rsqrt_ready")
        nm_ready, exp_ready, rs_ready, rr_ready = sem("nm_ready"), sem("exp_ready"), sem("rsum_ready"), sem("rrec_ready")
        xsF_ready, fsq_ready, rsd_ready, norm_ready, xn_ready, gelu_ready, xsA_ready = (sem(n) for n in (
            "xsF_ready", "f_sq_ready", "f_rsd_ready", "f_norm_ready", "f_xn_ready", "gelu_ready", "xsA_ready"))
        assert sems[-1].num - sems[0].num == len(sems) - 1

        def slot(kind, n):
            return PLACE[kind, n] % RING

        def read(kind, n):
            return drained[slot(kind, n)], PLACE[kind, n] // RING + 1

        def unit(kind, n):
            return ring[:, slot(kind, n), :]

        def by_rc(ap):
            return ap.rearrange("p (r c k) -> p r c k", r=2, c=NC)

        with nc.Block() as block:

            @block.gpsimd
            def _(pool):
                nc.gpsimd.memset(kT[:], 0.0).then_inc(kT_cleared, 1)
                pool.wait_ge(kT_cleared, 1)

        with nc.Fori(0, DEPTH) as layer:
            with nc.Block() as block:

                @block.sync
                def _(sp):
                    nxt = (layer + 1) % DEPTH
                    sp.wait_ge(filled["v1"], NT)
                    sp.wait_ge(rope_ready, 1)
                    wt.load_qkv(sp, nxt)
                    sp.wait_ge(filled["W"], NG)
                    wt.load_wo(sp, nxt)
                    sp.wait_ge(*read("y", NG - 1))
                    wt.load_ffn(sp, nxt)

                @block.gpsimd
                def _(pool):
                    pool.wait_ge(wt.qkv_loaded, (layer + 1) * wt.QKV)
                    for x in range(2):
                        nc.gpsimd.tensor_tensor(rope[:, x, 0, :, :], c.rope[:, :, 2 * x, :],
                                                wt.scales[:, x, None, :].broadcast_to([P, QT, DH]), ALU.mult).then_inc(rope_step, 1)
                        for half in range(2):
                            mine, other = slice(32 * half, 32 * half + 32), slice(32 - 32 * half, 64 - 32 * half)
                            nc.gpsimd.tensor_tensor(rope[:, x, 1, :, mine], c.rope[:, :, 2 * x + 1, mine],
                                                    wt.scales[:, x, None, other].broadcast_to([P, QT, DH // 2]), ALU.mult).then_inc(rope_step, 1)
                    pool.wait_ge(rope_step, 6)
                    pool.sem_inc(rope_ready, 1)
                    for t in range(NT):
                        for x in range(2):
                            pool.wait_ge(t1_ready[x], t + 1)
                            pool.wait_ge(t2_ready[x], t + 1)
                            nc.gpsimd.tensor_tensor(rot[:, x, :], rot[:, x, :], rot2[:, x, :], ALU.add).then_inc(rot_ready[x], 1)
                        pool.wait_ge(rsqrt_ready, t + 1)
                        pool.wait_ge(rot_ready[1], t + 1)
                        kv = rot[:, 1, :].rearrange("p (h d) -> p h d", h=HEADS)
                        nc.gpsimd.tensor_tensor(kv, kv, yv[:, HEADS:, None].broadcast_to([P, HEADS, DH]),
                                                ALU.mult).then_inc(unit_ready[1], 1)

                @block.scalar
                def _(act):
                    def evacuate(kind, n, out, in_=None):
                        act.wait_ge(filled[kind], n + 1)
                        nc.scalar.activation(out, unit(kind, n) if in_ is None else in_, ACT.Copy).then_inc(drained[slot(kind, n)], 1)

                    for kind, n in ORDER:
                        if kind in ("q", "k"):
                            x = "qk".index(kind)
                            if n >= 1:
                                act.wait_ge(t1_ready[x], n)
                                act.wait_ge(t2_ready[x], n)
                            evacuate(kind, n, raw[:, x, :])
                            act.wait_ge(*read(kind, n))
                            if n >= 1:
                                act.wait_ge(ss_ready, 2 * (n - 1) + x + 1)
                            nc.scalar.activation(sqr[:, x, :], raw[:, x, :], ACT.Square).then_inc(sq_ready[x], 1)
                        elif kind in ("v0", "v1"):
                            j = 2 * int(kind[1])
                            if n >= 2:
                                act.wait_ge(filled["O"], n - 1)
                            evacuate(kind, n, v[:, n % 2, j:j + 2, :, :].rearrange("p j c d -> p (j c d)"))
                        elif kind == "qT":
                            if n >= 1:
                                act.wait_ge(filled["S"], n)
                            evacuate(kind, n, qT[:].rearrange("p c t -> p (c t)"))
                        elif kind == "kT":
                            src = unit(kind, n).rearrange("p (c t) -> p c t", c=NC)
                            if n >= 1:
                                act.wait_ge(filled["S"], n)
                            act.wait_ge(filled[kind], n + 1)
                            nc.scalar.activation(kT[:, :, n % 2, WIN:], src, ACT.Copy)
                            lead = src[:, :, P - WIN:] if (n + 1) % QT else c.xsA[:, None, 0:XPAD].broadcast_to([P, NC, WIN])
                            nc.scalar.activation(kT[:, :, (n + 1) % 2, 0:WIN], lead, ACT.Copy).then_inc(drained[slot(kind, n)], 1)
                        elif kind == "S":
                            act.wait_ge(*read(kind, n))
                            nc.scalar.activation(prob[:], prob[:], ACT.Exp, scale=8.0).then_inc(exp_ready, 1)
                        elif kind == "PT":
                            if n >= 1:
                                act.wait_ge(filled["O"], n)
                            evacuate(kind, n, pT[:].rearrange("p c t -> p (c t)"))
                        elif kind == "OT":
                            if n % TPG == 0 and n:
                                act.wait_ge(filled["W"], n // TPG)
                            evacuate(kind, n, oT[:, :, (n % TPG) * P:(n % TPG + 1) * P],
                                     unit(kind, n).rearrange("p (c t) -> p c t", c=NC))
                        elif kind == "mean":
                            act.wait_ge(*read(kind, n))
                            if n >= 2:
                                act.wait_ge(filled["var"], n - 1)
                            nc.scalar.activation(sq[:, n % 2, :], xc[:, n % 2, :], ACT.Square).then_inc(fsq_ready, 1)
                        elif kind == "var":
                            act.wait_ge(filled["var"], n + 1)
                            if n >= 2:
                                act.wait_ge(norm_ready, n - 1)
                            nc.scalar.activation(sd[:, n % 2, :], unit(kind, n)[:, 0:GT], ACT.Sqrt,
                                                 bias=c.eps[:, 0:1]).then_inc(drained[slot(kind, n)], 1)
                        elif kind[0] == "h":
                            ch, m = int(kind[1]), HIDDEN[kind, n]
                            sz = FCH[ch][1]
                            act.wait_ge(filled[kind], n + 1)
                            if m == 0:
                                act.wait_ge(wt.ffn_loaded, (layer + 1) * wt.FFN)
                            if m >= 2:
                                act.wait_ge(*read(*[u for u in HIDDEN if HIDDEN[u] == m - 2][0]))
                            nc.scalar.activation(gl[0:sz, m % 2, :], unit(kind, n)[0:sz, 0:GT], ACT.Gelu,
                                                 bias=wt.b1[0:sz, 1, ch:ch + 1]).then_inc(gelu_ready, 1)

                @block.vector
                def _(dve):
                    steps = [0]

                    def step(ins):
                        steps[0] += 1
                        ins.then_inc(rsqrt_step, 1)
                        dve.wait_ge(rsqrt_step, steps[0])

                    def rotate(t, x):
                        def heads(ap):
                            return ap.rearrange("p (h e d) -> p h e d", h=HEADS, e=2)

                        def table(i):
                            return rope[:, x, i, t % QT, :].rearrange("p (o e d) -> p o e d", o=1, e=2).broadcast_to([P, HEADS, 2, DH // 2])

                        dve.wait_ge(*read("qk"[x], t))
                        if t == 0 and x == 0:
                            dve.wait_ge(rope_ready, 1)
                        if t >= 1:
                            dve.wait_ge(filled["qT" if x == 0 else "kT"], t)
                            dve.wait_ge(rot_ready[x], t)
                        nc.vector.tensor_tensor(heads(rot[:, x, :]), heads(raw[:, x, :]), table(0), ALU.mult).then_inc(t1_ready[x], 1)
                        nc.vector.tensor_tensor(heads(rot2[:, x, :]), heads(raw[:, x, :])[:, :, ::-1, :], table(1), ALU.mult).then_inc(t2_ready[x], 1)

                    def soft(n):
                        dve.wait_ge(filled["S"], n + 1)
                        nc.vector.tensor_reduce(nm[:], by_rc(unit("S", n)), AX.X, ALU.max, negate=True).then_inc(nm_ready, 1)
                        dve.wait_ge(nm_ready, n + 1)
                        if n >= 1:
                            dve.wait_ge(filled["PT"], n)
                        nc.vector.tensor_tensor(prob[:].rearrange("p c r k -> p r c k"), by_rc(unit("S", n)),
                                                nm[:, :, :, None].broadcast_to([P, 2, NC, 2 * WIN]), ALU.add).then_inc(drained[slot("S", n)], 1)

                    def lengths(t):
                        for x in range(2):
                            dve.wait_ge(sq_ready[x], t + 1)
                            nc.vector.tensor_reduce(ss[:, x * HEADS:(x + 1) * HEADS], sqr[:, x, :].rearrange("p (h d) -> p h d", h=HEADS),
                                                    AX.X, ALU.add).then_inc(ss_ready, 1)
                        dve.wait_ge(ss_ready, 2 * t + 2)
                        if t >= 1:
                            dve.wait_ge(unit_ready[1], t)
                        step(nc.vector.tensor_scalar(ss[:], ss[:], 1e-24, None, ALU.max))
                        step(nc.vector.tensor_scalar(yv[:].bitcast(I32), ss[:].bitcast(I32), 1, None, ALU.logical_shift_right))
                        step(nc.vector.tensor_scalar(yv[:].bitcast(I32), yv[:].bitcast(I32), -1.0, float(RSQRT_MAGIC), ALU.mult, ALU.add))
                        for it in range(3):
                            step(nc.vector.tensor_tensor(tv[:], ss[:], yv[:], ALU.mult))
                            step(nc.vector.scalar_tensor_tensor(uv[:], tv[:], -0.5, yv[:], ALU.mult, ALU.mult))
                            last = nc.vector.scalar_tensor_tensor(yv[:], uv[:], 1.5, yv[:], ALU.add, ALU.mult)
                            if it < 2:
                                step(last)
                        last.then_inc(rsqrt_ready, 1)

                    def unit_q(t):
                        dve.wait_ge(rot_ready[0], t + 1)
                        dve.wait_ge(rsqrt_ready, t + 1)
                        qv = rot[:, 0, :].rearrange("p (h d) -> p h d", h=HEADS)
                        nc.vector.tensor_tensor(qv, qv, yv[:, 0:HEADS, None].broadcast_to([P, HEADS, DH]), ALU.mult).then_inc(unit_ready[0], 1)

                    def sums(n):
                        dve.wait_ge(exp_ready, n + 1)
                        nc.vector.tensor_reduce(rs[:], prob[:], AX.X, ALU.add).then_inc(rs_ready, 1)
                        dve.wait_ge(rs_ready, n + 1)
                        nc.vector.reciprocal(rr[:], rs[:]).then_inc(rr_ready, 1)

                    def normalise(n):
                        dve.wait_ge(rr_ready, n + 1)
                        dve.wait_ge(filled["O"], n + 1)
                        if n >= 1:
                            dve.wait_ge(filled["OT"], n)
                        nc.vector.tensor_tensor(o[:], by_rc(unit("O", n)).rearrange("p r c d -> p c r d"),
                                                rr[:, :, :, None].broadcast_to([P, NC, 2, DH]), ALU.mult).then_inc(drained[slot("O", n)], 1)

                    for kind, n in ORDER:
                        s = drained[slot(kind, n)]
                        g = slice(n * GT, (n + 1) * GT)
                        if kind == "k":
                            rotate(n, 0)
                            rotate(n, 1)
                            if n == 0:
                                lengths(0)
                                unit_q(0)
                        elif kind == "S":
                            soft(n)
                            if n + 1 < NT:
                                lengths(n + 1)
                            sums(n)
                        elif kind == "O":
                            if n + 1 < NT:
                                unit_q(n + 1)
                            normalise(n)
                        elif kind == "W":
                            dve.wait_ge(filled[kind], n + 1)
                            nc.vector.tensor_tensor(c.xT[:, g], unit(kind, n)[:, 0:GT], c.xT[:, g], ALU.add).then_inc(s, 1)
                            dve.wait_ge(*read(kind, n))
                            shift_copy(nc, c.xT, c.xsF, n).then_inc(xsF_ready, 1)
                        elif kind == "mean":
                            col = xcol(n * GT)
                            dve.wait_ge(filled[kind], n + 1)
                            nc.vector.tensor_tensor(xc[:, n % 2, :], c.xsF[:, col:col + GT], unit(kind, n)[:, 0:GT], ALU.subtract).then_inc(s, 1)
                        elif kind == "var":
                            dve.wait_ge(*read(kind, n))
                            nc.vector.reciprocal(sd[:, n % 2, :], sd[:, n % 2, :]).then_inc(rsd_ready, 1)
                            dve.wait_ge(rsd_ready, n + 1)
                            if n >= 2:
                                dve.wait_ge(filled["h2"], n - 1)
                            nc.vector.tensor_tensor(xn[:, n % 2, :], xc[:, n % 2, :], sd[:, n % 2, :], ALU.mult).then_inc(norm_ready, 1)
                            dve.wait_ge(norm_ready, n + 1)
                            if n == 0:
                                dve.wait_ge(wt.ffn_loaded, (layer + 1) * wt.FFN)
                            nc.vector.tensor_scalar(xn[:, n % 2, :], xn[:, n % 2, :], wt.lg[:, 0:1], wt.lb[:, 0:1], ALU.mult, ALU.add).then_inc(xn_ready, 1)
                        elif kind[0] == "h":
                            ch, m = int(kind[1]), HIDDEN[kind, n]
                            sz = FCH[ch][1]
                            dve.wait_ge(gelu_ready, m + 1)
                            if n >= 2:
                                dve.wait_ge(filled["y"], n - 1)
                            nc.vector.scalar_tensor_tensor(hh[0:sz, n % 2, ch, :], unit(kind, n)[0:sz, GT:], wt.b1[0:sz, 0, ch:ch + 1],
                                                           gl[0:sz, m % 2, :], ALU.add, ALU.mult).then_inc(s, 1)
                        elif kind == "y":
                            dve.wait_ge(filled[kind], n + 1)
                            nc.vector.scalar_tensor_tensor(c.xT[:, g], unit(kind, n)[:, 0:GT], wt.b2[:, 0:1], c.xT[:, g],
                                                           ALU.add, ALU.add).then_inc(s, 1)
                            dve.wait_ge(*read(kind, n))
                            shift_copy(nc, c.xT, c.xsA, n).then_inc(xsA_ready, 1)
                    dve.wait_ge(xsA_ready, NG)

                @block.tensor
                def _(pe):
                    for kind, n in ORDER:
                        u = PLACE[kind, n]
                        if u >= RING:
                            pe.wait_ge(drained[u % RING], u // RING)
                        ps = unit(kind, n)
                        if kind in ("q", "k"):
                            if kind == "q" and n == 0:
                                pe.wait_ge(wt.qkv_loaded, (layer + 1) * wt.QKV)
                            x = "qk".index(kind)
                            col = xcol(n * P)
                            for h in range(2):
                                f = x * INNER + h * GT
                                m = nc.tensor.matmul(ps[:, h * GT:(h + 1) * GT], c.xsA[:, col:col + P], wt.qkv[:, f:f + GT], start=True, stop=True)
                        elif kind in ("v0", "v1"):
                            wv = wt.qkv[:, 2 * INNER:].rearrange("p (c r d) -> p r c d", r=2, c=NC)
                            for jj in range(2):
                                col = xcol(n * P + (2 * int(kind[1]) + jj) * WIN) - WIN
                                for r in range(2):
                                    m = nc.tensor.matmul(ps[64 * r:64 * r + 64, jj * GT:(jj + 1) * GT], c.xsA[:, col:col + 2 * WIN],
                                                         wv[:, r, :, :], start=True, stop=True)
                        elif kind in ("qT", "kT"):
                            x = "qk".index(kind[0])
                            pe.wait_ge(unit_ready[x], n + 1)
                            for ch in range(NC):
                                m = nc.tensor.transpose(ps[:, ch * P:(ch + 1) * P], rot[:, x, ch * P:(ch + 1) * P], c.ident[:])
                        elif kind == "S":
                            pe.wait_ge(*read("qT", n))
                            pe.wait_ge(*read("kT", n))
                            first_tile = int(n % QT == 0)
                            for r in range(2):
                                nc.tensor.matmul(ps[:, r * GT:(r + 1) * GT], c.identb[:],
                                                 c.mask[:, first_tile, None, :].broadcast_to([P, NC, 2 * WIN]),
                                                 start=True, stop=False, skip_group_check=True)
                            for ch in range(NC):
                                for r in range(2):
                                    for j in range(WPT):
                                        m = nc.tensor.matmul(
                                            ps[32 * j:32 * j + 32, r * GT + ch * 64:r * GT + ch * 64 + 64],
                                            qT[64 * r:64 * r + 64, ch, 32 * j:32 * j + 32],
                                            kT[64 * r:64 * r + 64, ch, n % 2, 32 * j:32 * j + 64],
                                            start=False, stop=(ch == NC - 1), skip_group_check=True)
                        elif kind == "PT":
                            pe.wait_ge(exp_ready, n + 1)
                            for ch in range(NC):
                                m = nc.tensor.transpose(ps[:, ch * P:(ch + 1) * P], prob[:, ch, :, :].rearrange("p r k -> p (r k)"), c.ident[:])
                        elif kind == "O":
                            for part in ("PT", "v0", "v1"):
                                pe.wait_ge(*read(part, n))
                            for ch in range(NC):
                                for r in range(2):
                                    for j in range(WPT):
                                        m = nc.tensor.matmul(
                                            ps[32 * j:32 * j + 32, r * GT + ch * 64:r * GT + ch * 64 + 64],
                                            pT[64 * r:64 * r + 64, ch, 32 * j:32 * j + 32],
                                            v[64 * r:64 * r + 64, n % 2, j, ch, :], start=True, stop=True)
                        elif kind == "OT":
                            pe.wait_ge(*read("O", n))
                            for ch in range(NC):
                                m = nc.tensor.transpose(ps[:, ch * P:(ch + 1) * P], o[:, ch, :, :].rearrange("p r d -> p (r d)"), c.ident[:])
                        elif kind == "W":
                            pe.wait_ge(*read("OT", n * TPG + TPG - 1))
                            if n == 0:
                                pe.wait_ge(wt.wo_loaded, (layer + 1) * wt.WO)
                            for ch in range(NC):
                                m = nc.tensor.matmul(ps[:, 0:GT], wt.wo[:, ch, :], oT[:, ch, :], start=(ch == 0), stop=(ch == NC - 1))
                        elif kind == "mean":
                            pe.wait_ge(xsF_ready, n + 1)
                            col = xcol(n * GT)
                            m = nc.tensor.matmul(ps[:, 0:GT], c.ones_d[:], c.xsF[:, col:col + GT], start=True, stop=True)
                        elif kind == "var":
                            pe.wait_ge(fsq_ready, n + 1)
                            m = nc.tensor.matmul(ps[:, 0:GT], c.ones_d[:], sq[:, n % 2, :], start=True, stop=True)
                        elif kind[0] == "h":
                            off, sz = FCH[int(kind[1])]
                            pe.wait_ge(xn_ready, n + 1)
                            nc.tensor.matmul(ps[0:sz, 0:GT], wt.w1[:, F + off:F + off + sz], xn[:, n % 2, :], start=True, stop=True)
                            m = nc.tensor.matmul(ps[0:sz, GT:], wt.w1[:, off:off + sz], xn[:, n % 2, :], start=True, stop=True)
                        elif kind == "y":
                            for ch, (off, sz) in enumerate(FCH):
                                pe.wait_ge(*read(f"h{ch}", n))
                                m = nc.tensor.matmul(ps[:, 0:GT], wt.w2[0:sz, ch, :], hh[0:sz, n % 2, ch, :], start=(ch == 0), stop=(ch == len(FCH) - 1))
                        m.then_inc(filled[kind], 1)

            nc.all_engine_barrier()
            nc.gpsimd.sem_clear(range(sems[0].num, sems[-1].num + 1))
            nc.all_engine_barrier()


def finish(nc, c, wt, out):
    with ExitStack() as ctx:
        sb = lambda n, s, d=F32: ctx.enter_context(nc.sbuf_tensor(n, s, d))
        sem = lambda n: ctx.enter_context(nc.semaphore(n))
        ps = ctx.enter_context(nc.psum_tensor("fin_ps", [P, 8, GT], F32))
        xc, sq, sd, y, z, rows = (sb(n, [P, T]) for n in ("e_xc", "e_sq", "e_sd", "e_y", "e_z", "e_rows"))
        mean, xcr, sqr, var, sdr, rs, done = (sem(f"e_{n}") for n in ("mean", "xc", "sq", "var", "sd", "rs", "ln"))
        x_there, z_ready, zT_filled, rows_ready, stored = (sem(n) for n in ("x_there", "z_ready", "zT_filled", "rows_ready", "out_stored"))
        with nc.Block() as block:

            @block.sync
            def _(sp):
                for g in range(NG):
                    sp.wait_ge(rows_ready, g + 1)
                    sp.dma_start(out[g // 2, (g % 2) * GT:(g % 2 + 1) * GT, :].rearrange("(t p) d -> p t d", p=P),
                                 rows[:, g * GT:(g + 1) * GT].rearrange("p (t d) -> p t d", t=TPG)).then_inc(stored, 16)
                sp.wait_ge(stored, 16 * NG)
                sp.wait_ge(wt.qkv_loaded, (DEPTH + 1) * wt.QKV)
                sp.wait_ge(wt.wo_loaded, (DEPTH + 1) * wt.WO)
                sp.wait_ge(wt.ffn_loaded, (DEPTH + 1) * wt.FFN)

            @block.tensor
            def _(pe):
                pe.sem_inc(x_there, NG)
                layer_norm_pe(nc, pe, c.ones_d, grp(c.xT), grp(sq), lambda g: ps[:, g, :], lambda g: ps[:, 4 + g, :],
                              x_there, sqr, mean, var)
                for g in range(NG):
                    pe.wait_ge(z_ready, g + 1)
                    for j in range(TPG):
                        t = g * TPG + j
                        m = nc.tensor.transpose(ps[:, g, j * P:(j + 1) * P], z[:, t * P:(t + 1) * P], c.ident[:])
                    m.then_inc(zT_filled, 1)

            @block.scalar
            def _(act):
                layer_norm_act(nc, act, c.eps, grp(xc), grp(sq), lambda g: ps[:, 4 + g, :], grp(sd), xcr, sqr, var, sdr)
                for g in range(NG):
                    act.wait_ge(zT_filled, g + 1)
                    nc.scalar.activation(grp(rows)(g), ps[:, g, :], ACT.Copy).then_inc(rows_ready, 1)

            @block.vector
            def _(dve):
                layer_norm_dve(nc, dve, grp(c.xT), grp(xc), lambda g: ps[:, g, :], grp(sd), grp(y), mean, xcr, sdr, rs, done)
                for g in range(NG):
                    dve.wait_ge(done, g + 1)
                    nc.vector.tensor_tensor(grp(z)(g), grp(c.x1)(g), grp(y)(g), ALU.add).then_inc(z_ready, 1)


class Chip:

    def __init__(self, nc, ctx, ident, rope, mask):
        sb = lambda n, s, d=F32: ctx.enter_context(nc.sbuf_tensor(n, s, d))
        self.ident_dram, self.rope_dram, self.mask_dram = ident, rope, mask
        self.ident, self.identb = sb("ident", [P, P]), sb("identb", [P, P], BF16)
        self.ones_d, self.eps = sb("ones_d", [P, P]), sb("eps", [P, 1])
        self.mask32, self.mask = sb("mask32", [P, 2, 2 * WIN]), sb("mask", [P, 2, 2 * WIN], BF16)
        self.rope = sb("rope", [P, QT, 4, DH])
        self.x0, self.xT = sb("x0", [P, T]), sb("xT", [P, T])
        self.x1 = self.x0
        self.xsA, self.xsF = sb("xsA", [P, B * XB]), sb("xsF", [P, B * XB])


def program(nc, x, wqkv1, wproj, bproj, wqkv, qs, ks, wo, lg, lb, w1, b1, w2, b2, ident, rope, mask, out):
    with ExitStack() as ctx:
        c = Chip(nc, ctx, ident, rope, mask)
        wt = Weights(nc, ctx, wqkv, qs, ks, wo, lg, lb, w1, b1, w2, b2)
        with nc.sbuf_tensor("o_tok", [P, NT, D], F32) as c.o_tok:
            load_and_project(nc, c, x, wqkv1)
            project(nc, c, wproj, bproj, wt)
        layers(nc, c, wt)
        finish(nc, c, wt, out)


def constants():
    import numpy as np
    f = np.float32
    half = np.arange(0, DH, 2, dtype=f)
    inv = (f(1.0) / np.power(f(10000.0), half / f(DH))).astype(f)
    t = np.arange(N, dtype=f)
    ang = (t[:, None] * inv[None, :]).astype(f)
    base = ((half + f(0.4 * DH)) / f(1.4 * DH)).astype(f)
    power = ((t - f(N // 2)) / f(WIN // 2)).astype(f)
    scale = np.power(base[None, :], power[:, None]).astype(f)
    cos, sin = np.cos(ang).astype(f), np.sin(ang).astype(f)
    rec = (f(1.0) / scale).astype(f)
    tab = np.stack([np.concatenate([a, b], -1) for a, b in (
        (cos * scale, cos * scale), (-sin * scale, sin * scale), (cos * rec, cos * rec), (-sin * rec, sin * rec))], 1)
    tab = np.ascontiguousarray(tab.reshape(QT, P, 4, DH).transpose(1, 0, 2, 3)).astype(f)
    i, j = np.arange(P)[:, None] % WIN, np.arange(2 * WIN)[None, :] - WIN
    ordinary = np.where((j > i) | (i > j + WIN), f(NEG), f(0))
    start = np.where((np.arange(P)[:, None] < WIN) & (j < 0), f(NEG), ordinary)
    return np.eye(P, dtype=f), tab, np.ascontiguousarray(np.stack([ordinary, start], 1)).astype(f)


_INS = ["L0_attn_x", "L0_attn_Wqkv", "L0_attn_Wproj", "L0_attn_bproj", "L0_ffn_Wqkv", "L0_ffn_q_scale", "L0_ffn_k_scale",
        "L0_ffn_Wo", "L0_ffn_ln_g", "L0_ffn_ln_b", "L0_ffn_W1", "L0_ffn_b1", "L0_ffn_W2", "L0_ffn_b2"]


def kernel(**inputs):
    import numpy as _np
    import concourse.bacc as _bacc
    from concourse import mybir as _mybir
    from concourse.bass_utils import run_bass_kernel_spmd as _run

    nc = _bacc.Bacc("TRN2", target_bir_lowering=False, num_devices=1)
    arrays, args = {}, []
    ident, rope, mask = constants()
    for name, a in [(n, inputs[n]) for n in _INS] + [("ident", ident), ("rope", rope), ("mask", mask)]:
        a = _np.ascontiguousarray(a)
        arrays[f"in_{name}"] = a
        args.append(nc.dram_tensor(f"in_{name}", a.shape, _mybir.dt.from_np(a.dtype), kind="ExternalInput").ap())
    args.append(nc.dram_tensor("out", (B, N, D), _mybir.dt.float32, kind="ExternalOutput").ap())
    program(nc, *args)
    r = _run(nc, [arrays], core_ids=[0])
    return r.results[0]["out"]
```

```python
from contextlib import ExitStack

import concourse.bass as bass
from concourse import mybir

F32 = mybir.dt.float32
BF16 = mybir.dt.bfloat16
I32 = mybir.dt.int32
ALU = mybir.AluOpType
ACT = mybir.ActivationFunctionType
AX = mybir.AxisListType

P = 128
B, N, D = 2, 1024, 128
T = B * N
GT = 512
NG = T // GT
NT = T // P
EPS = 1e-5

H1, D1 = 16, 8
QT = N // P

DEPTH, HEADS, DH, WIN = 6, 16, 64, 32
INNER = HEADS * DH
NC = INNER // P
F = 341
FCH = [(0, 128), (128, 128), (256, F - 256)]
NEG = -1e30
RSQRT_MAGIC = 0x5F3759DF
TPG = GT // P
WPT = P // WIN
XPAD = WIN
XB = XPAD + N + 1


def xcol(t0):
    return (t0 // N) * XB + XPAD + t0 % N


def layer_norm_pe(nc, pe, ones_d, src, sq, ps_mean, ps_var, src_ready, sq_ready, mean_ready, var_ready):
    for g in range(NG):
        pe.wait_ge(src_ready, g + 1)
        nc.tensor.matmul(ps_mean(g), ones_d[:], src(g), start=True, stop=True).then_inc(mean_ready, 1)
    for g in range(NG):
        pe.wait_ge(sq_ready, g + 1)
        nc.tensor.matmul(ps_var(g), ones_d[:], sq(g), start=True, stop=True).then_inc(var_ready, 1)


def layer_norm_act(nc, act, eps, xc, sq, ps_var, sd, xc_ready, sq_ready, var_ready, sd_ready):
    for g in range(NG):
        act.wait_ge(xc_ready, g + 1)
        nc.scalar.activation(sq(g), xc(g), ACT.Square).then_inc(sq_ready, 1)
    for g in range(NG):
        act.wait_ge(var_ready, g + 1)
        nc.scalar.activation(sd(g), ps_var(g), ACT.Sqrt, bias=eps[:, 0:1]).then_inc(sd_ready, 1)


def layer_norm_dve(nc, dve, src, xc, ps_mean, sd, out, mean_ready, xc_ready, sd_ready, rs_ready, ln_ready):
    for g in range(NG):
        dve.wait_ge(mean_ready, g + 1)
        nc.vector.tensor_tensor(xc(g), src(g), ps_mean(g), ALU.subtract).then_inc(xc_ready, 1)
    for g in range(NG):
        dve.wait_ge(sd_ready, g + 1)
        nc.vector.reciprocal(sd(g), sd(g)).then_inc(rs_ready, 1)
        dve.wait_ge(rs_ready, g + 1)
        nc.vector.tensor_tensor(out(g), xc(g), sd(g), ALU.mult).then_inc(ln_ready, 1)


def grp(t):
    return lambda g: t[:, g * GT:(g + 1) * GT]


def load_and_project(nc, c, x, wqkv, weights):
    HV = 9
    QKV = 3 * H1 * D1
    with ExitStack() as ctx:
        sb = lambda n, s, d=F32: ctx.enter_context(nc.sbuf_tensor(n, s, d))
        sem = lambda n: ctx.enter_context(nc.semaphore(n))
        ps = ctx.enter_context(nc.psum_tensor("prep_ps", [P, 8, GT], F32))
        xin = sb("xin", [P, NT, D])
        win = sb("win", [P, 3, D])
        wT = sb("wT", [P, QKV])
        xc, sq, sd, xn = (sb(n, [P, T]) for n in ("xc", "sq", "sd", "xn"))
        qkv = sb("qkv", [P, 4, H1, 3, D1])
        qk_prod = sb("qk_prod", [P, 2, H1, H1, D1])
        pv_prod = sb("pv_prod", [P, 2, H1, D1, H1])
        prob = sb("prob", [P, 2, H1, H1])
        nmax, den = sb("nmax", [P, H1]), sb("den", [P, H1])
        num = sb("num", [P, H1, D1])
        x_loaded, w_loaded, const_loaded = sem("x_loaded"), sem("w_loaded"), sem("p_const_loaded")
        eps_ready, xT_filled, wT_filled, x0_ready = sem("eps_ready"), sem("xT_filled"), sem("wT_filled"), sem("x0_ready")
        wT_ready = sem("wT_ready")
        mean_ready, xc_ready, sq_ready, var_ready = sem("mean_ready"), sem("xc_ready"), sem("sq_ready"), sem("var_ready")
        sd_ready, rs_ready, ln_ready = sem("sd_ready"), sem("rs_ready"), sem("ln_ready")
        qkv_filled, qkv_ready, qk_multiplied, scored = sem("qkv_filled"), sem("qkv_ready"), sem("qk_multiplied"), sem("scored")
        maxed, centred, exped, pv_pool, pv_dve = sem("maxed"), sem("centred"), sem("exped"), sem("pv_pool"), sem("pv_dve")
        den_step, pv_summed, o_ready = sem("den_step"), sem("pv_summed"), sem("o_ready")
        psf = ps[:].rearrange("p a b -> p (a b)")
        x_rows = x.rearrange("b (t p) d -> p (b t) d", p=P)

        def loop(eng, body):
            body(0, 0)
            with eng.Fori(0, 3) as i:
                for u in range(4):
                    body(i * 4 + (u + 1), u + 1)
            for t in range(13, NT + 1):
                body(t, t)

        with nc.Block() as block:

            @block.sync
            def _(sp):
                for h in range(2):
                    sp.dma_start(xin[:, 8 * h:8 * h + 8, :], x_rows[:, 8 * h:8 * h + 8, :]).then_inc(x_loaded, 16)
                sp.dma_start(c.rope[:], c.rope_dram).then_inc(const_loaded, 16)
                weights.load_scales(sp, 0)
                for part in range(3):
                    weights.load_qkv(sp, 0, part)
                weights.load_wo(sp, 0)
                weights.load_ffn(sp, 0)
                sp.wait_ge(const_loaded, 16)

            @block.gpsimd
            def _(pool):
                nc.gpsimd.memset(c.ones_d[:], 1.0 / D).then_inc(eps_ready, 1)
                nc.gpsimd.memset(c.eps[:], EPS).then_inc(eps_ready, 1)
                nc.gpsimd.memset(c.xsA[:], 0.0).then_inc(eps_ready, 1)
                nc.gpsimd.memset(c.xsF[:], 0.0).then_inc(eps_ready, 1)
                pool.wait_ge(eps_ready, 4)
                pool.sem_inc(pv_pool, 4)

                def body(t, k):
                    if k < NT:
                        pool.wait_ge(qkv_ready, t + 1)
                        pool.wait_ge(scored, t + 1)
                        q, kk = qkv[:, k % 4, :, 0, :], qkv[:, k % 4, :, 1, :]
                        nc.gpsimd.tensor_tensor(qk_prod[:, k % 2, :, :, :], q[:, :, None, :].broadcast_to([P, H1, H1, D1]),
                                                kk[:, None, :, :].broadcast_to([P, H1, H1, D1]), ALU.mult).then_inc(qk_multiplied, 1)
                    if k >= 1:
                        pool.wait_ge(exped, t)
                        pool.wait_ge(pv_summed, t)
                        v = qkv[:, (k - 1) % 4, :, 2, :].rearrange("p g d -> p d g")
                        nc.gpsimd.tensor_tensor(pv_prod[:, (k - 1) % 2, 0:HV, :, :],
                                                prob[:, (k - 1) % 2, 0:HV, None, :].broadcast_to([P, HV, D1, H1]),
                                                v[:, None, :, :].broadcast_to([P, HV, D1, H1]), ALU.mult).then_inc(pv_pool, 1)

                loop(pool, body)

            @block.scalar
            def _(act):
                act.dma_start(c.ident[:], c.ident_dram).then_inc(w_loaded, 16)
                act.dma_start(win[:], wqkv.rearrange("(a p) m -> p a m", p=P)).then_inc(w_loaded, 16)
                act.dma_start(c.mask32[:], c.mask_dram).then_inc(w_loaded, 16)
                act.wait_ge(wT_filled, 1)
                nc.scalar.activation(wT[:], psf[:, 4 * GT:4 * GT + QKV], ACT.Copy).then_inc(wT_ready, 1)
                act.wait_ge(eps_ready, 4)
                layer_norm_act(nc, act, c.eps, grp(xc), grp(sq), lambda g: ps[:, 4 + g, :], grp(sd),
                               xc_ready, sq_ready, var_ready, sd_ready)

                def body(t, k):
                    if k < NT:
                        act.wait_ge(qkv_filled, t + 1)
                        act.wait_ge(pv_pool, t + 1)
                        act.wait_ge(pv_dve, t + 1)
                        nc.scalar.activation(qkv[:, k % 4, :, :, :].rearrange("p h c d -> p (h c d)"), ps[:, k % 2, 0:QKV],
                                             ACT.Copy).then_inc(qkv_ready, 1)
                    if k >= 1:
                        act.wait_ge(centred, t)
                        nc.scalar.activation(prob[:, (k - 1) % 2, :, :], prob[:, (k - 1) % 2, :, :], ACT.Exp,
                                             scale=1.0 / 8.0).then_inc(exped, 1)

                loop(act, body)

            @block.vector
            def _(dve):
                for g in range(NG):
                    dve.wait_ge(xT_filled, g + 1)
                    nc.vector.tensor_copy(c.x0[:, g * GT:(g + 1) * GT], ps[:, g, :]).then_inc(x0_ready, 1)
                dve.wait_ge(w_loaded, 48)
                nc.vector.tensor_copy(c.identb[:], c.ident[:]).then_inc(x0_ready, 1)
                nc.vector.tensor_copy(c.mask[:], c.mask32[:]).then_inc(x0_ready, 1)
                dve.wait_ge(x0_ready, NG + 2)
                layer_norm_dve(nc, dve, grp(c.x0), grp(xc), lambda g: ps[:, g, :], grp(sd), grp(xn),
                               mean_ready, xc_ready, sd_ready, rs_ready, ln_ready)
                dve.sem_inc(scored, 2)
                dve.sem_inc(pv_summed, 2)
                dve.sem_inc(pv_dve, 4)
                dve.sem_inc(o_ready, 1)

                def body(t, k):
                    if k < NT:
                        pr = prob[:, k % 2, :, :]
                        dve.wait_ge(qk_multiplied, t + 1)
                        dve.wait_ge(pv_pool, t + 3)
                        nc.vector.tensor_reduce(pr, qk_prod[:, k % 2, :, :, :], AX.X, ALU.add).then_inc(scored, 1)
                        dve.wait_ge(scored, t + 3)
                        nc.vector.tensor_reduce(nmax[:], pr, AX.X, ALU.max, negate=True).then_inc(maxed, 1)
                        dve.wait_ge(maxed, t + 1)
                        nc.vector.tensor_tensor(pr, pr, nmax[:, :, None].broadcast_to([P, H1, H1]), ALU.add).then_inc(centred, 1)
                    if k >= 1:
                        pr = prob[:, (k - 1) % 2, :, :]
                        v = qkv[:, (k - 1) % 4, :, 2, :].rearrange("p g d -> p d g")
                        dve.wait_ge(exped, t)
                        nc.vector.tensor_tensor(pv_prod[:, (k - 1) % 2, HV:, :, :],
                                                pr[:, HV:, None, :].broadcast_to([P, H1 - HV, D1, H1]),
                                                v[:, None, :, :].broadcast_to([P, H1 - HV, D1, H1]), ALU.mult).then_inc(pv_dve, 1)
                        dve.wait_ge(o_ready, t)
                        nc.vector.tensor_reduce(den[:], pr, AX.X, ALU.add).then_inc(den_step, 1)
                        dve.wait_ge(pv_pool, t + 4)
                        dve.wait_ge(pv_dve, t + 4)
                        nc.vector.tensor_reduce(num[:], pv_prod[:, (k - 1) % 2, :, :, :], AX.X, ALU.add).then_inc(pv_summed, 1)
                        dve.wait_ge(den_step, 2 * t - 1)
                        nc.vector.reciprocal(den[:], den[:]).then_inc(den_step, 1)
                        dve.wait_ge(pv_summed, t + 2)
                        dve.wait_ge(den_step, 2 * t)
                        nc.vector.tensor_tensor(c.o_tok[:, bass.ds(t - 1, 1), :].rearrange("p o (h d) -> p (o h) d", h=H1), num[:],
                                                den[:, :, None].broadcast_to([P, H1, D1]), ALU.mult).then_inc(o_ready, 1)

                loop(dve, body)

            @block.tensor
            def _(pe):
                pe.wait_ge(w_loaded, 48)
                pe.wait_ge(x_loaded, 32)
                for a in range(3):
                    m = nc.tensor.transpose(ps[:, 4, a * P:(a + 1) * P], win[:, a, :], c.ident[:])
                m.then_inc(wT_filled, 1)
                for g in range(NG):
                    for j in range(TPG):
                        m = nc.tensor.transpose(ps[:, g, j * P:(j + 1) * P], xin[:, g * TPG + j, :], c.ident[:])
                    m.then_inc(xT_filled, 1)
                pe.wait_ge(eps_ready, 4)
                pe.wait_ge(x0_ready, NG)
                pe.wait_ge(wT_ready, 1)
                layer_norm_pe(nc, pe, c.ones_d, grp(c.x0), grp(sq), lambda g: ps[:, g, :],
                              lambda g: ps[:, 4 + g, :], x0_ready, sq_ready, mean_ready, var_ready)
                for t in range(NT):
                    pe.wait_ge(ln_ready, t // TPG + 1)
                    if t >= 2:
                        pe.wait_ge(qkv_ready, t - 1)
                    nc.tensor.matmul(ps[:, t % 2, 0:QKV], xn[:, t * P:(t + 1) * P], wT[:], start=True, stop=True).then_inc(qkv_filled, 1)


def shift_copy(nc, src, dst, g):
    col = xcol(g * GT)
    nc.vector.tensor_copy(dst[0:64, col:col + GT], src[0:64, g * GT:(g + 1) * GT])
    return nc.vector.tensor_copy(dst[64:P, col + 1:col + 1 + GT], src[64:P, g * GT:(g + 1) * GT])


def project(nc, c, wproj, bproj):
    with ExitStack() as ctx:
        sb = lambda n, s, d=F32: ctx.enter_context(nc.sbuf_tensor(n, s, d))
        sem = lambda n: ctx.enter_context(nc.semaphore(n))
        ps = ctx.enter_context(nc.psum_tensor("proj_ps", [P, 8, GT], F32))
        w_in, wT, bp = sb("wp_in", [P, P]), sb("wpT", [P, P]), sb("bp", [P, 1])
        oT, a, xc, sq, sd, y = (sb(n, [P, T]) for n in ("oT", "attn", "c_xc", "c_sq", "c_sd", "c_y"))
        wp_loaded, oT_filled, oT_ready, wpT_filled, wpT_ready = (sem(n) for n in (
            "wp_loaded", "oT_filled", "oT_ready", "wpT_filled", "wpT_ready"))
        proj_filled, attn_ready, x1_ready, xT_shifted = sem("proj_filled"), sem("attn_ready"), sem("x1_ready"), sem("xT_shifted")
        ln = [[sem(f"c{r}_{n}") for n in ("mean", "xc", "sq", "var", "sd", "rs", "ln")] for r in range(2)]
        ps_mean, ps_var = lambda g: ps[:, g, :], lambda g: ps[:, 4 + g, :]
        with nc.Block() as block:

            @block.sync
            def _(sp):
                sp.dma_start(w_in[:], wproj).then_inc(wp_loaded, 16)
                sp.dma_start(bp[:], bproj.rearrange("(p o) -> p o", o=1)).then_inc(wp_loaded, 16)

            @block.tensor
            def _(pe):
                pe.wait_ge(wp_loaded, 32)
                nc.tensor.transpose(ps[:, 4, 0:P], w_in[:], c.ident[:]).then_inc(wpT_filled, 1)
                for g in range(NG):
                    for j in range(TPG):
                        m = nc.tensor.transpose(ps[:, g, j * P:(j + 1) * P], c.o_tok[:, g * TPG + j, :], c.ident[:])
                    m.then_inc(oT_filled, 1)
                pe.wait_ge(wpT_ready, 1)
                for g in range(NG):
                    pe.wait_ge(oT_ready, g + 1)
                    nc.tensor.matmul(ps[:, 4 + g, :], wT[:], oT[:, g * GT:(g + 1) * GT], start=True, stop=True).then_inc(proj_filled, 1)
                mean, xcr, sqr, var, sdr, rs, done = ln[0]
                pe.wait_ge(attn_ready, NG)
                layer_norm_pe(nc, pe, c.ones_d, grp(a), grp(sq), ps_mean, ps_var, attn_ready, sqr, mean, var)
                mean, xcr, sqr, var, sdr, rs, done = ln[1]
                layer_norm_pe(nc, pe, c.ones_d, grp(c.x1), grp(sq), ps_mean, ps_var, x1_ready, sqr, mean, var)

            @block.scalar
            def _(act):
                act.wait_ge(wpT_filled, 1)
                nc.scalar.activation(wT[:], ps[:, 4, 0:P], ACT.Copy).then_inc(wpT_ready, 1)
                for g in range(NG):
                    act.wait_ge(oT_filled, g + 1)
                    nc.scalar.activation(oT[:, g * GT:(g + 1) * GT], ps[:, g, :], ACT.Copy).then_inc(oT_ready, 1)
                for r in range(2):
                    mean, xcr, sqr, var, sdr, rs, done = ln[r]
                    layer_norm_act(nc, act, c.eps, grp(xc), grp(sq), ps_var, grp(sd), xcr, sqr, var, sdr)

            @block.vector
            def _(dve):
                dve.wait_ge(wp_loaded, 32)
                for g in range(NG):
                    dve.wait_ge(proj_filled, g + 1)
                    nc.vector.tensor_scalar(a[:, g * GT:(g + 1) * GT], ps[:, 4 + g, :], bp[:, 0:1], None, ALU.add).then_inc(attn_ready, 1)
                dve.wait_ge(attn_ready, NG)
                mean, xcr, sqr, var, sdr, rs, done = ln[0]
                layer_norm_dve(nc, dve, grp(a), grp(xc), ps_mean, grp(sd), grp(y), mean, xcr, sdr, rs, done)
                for g in range(NG):
                    dve.wait_ge(done, g + 1)
                    nc.vector.tensor_tensor(grp(c.x1)(g), grp(c.x1)(g), grp(y)(g), ALU.add).then_inc(x1_ready, 1)
                dve.wait_ge(x1_ready, NG)
                mean, xcr, sqr, var, sdr, rs, done = ln[1]
                layer_norm_dve(nc, dve, grp(c.x1), grp(xc), ps_mean, grp(sd), grp(c.xT), mean, xcr, sdr, rs, done)
                for g in range(NG):
                    dve.wait_ge(done, g + 1)
                    shift_copy(nc, c.xT, c.xsA, g).then_inc(xT_shifted, 1)
                dve.wait_ge(xT_shifted, NG)


class Weights:
    SCALES, QK, V, WO, FFN = 32, 32, 16, 16, 16 * 13

    def __init__(self, nc, ctx, wqkv, qs, ks, wo, lg, lb, w1, b1, w2, b2):
        sb = lambda n, s, d=F32: ctx.enter_context(nc.sbuf_tensor(n, s, d))
        self.dram = (wqkv, qs, ks, wo, lg, lb, w1, b1, w2, b2)
        self.qkv, self.wo = sb("w_qkv", [P, 3 * INNER]), sb("w_o", [P, NC, D])
        self.scales = sb("qk_scales", [P, 2, DH])
        self.lg, self.lb, self.b2 = sb("ln_g", [P, 1]), sb("ln_b", [P, 1]), sb("b2", [P, 1])
        self.w1, self.b1, self.w2 = sb("w1", [P, 2 * F]), sb("b1", [P, 2, len(FCH)]), sb("w2", [P, len(FCH), D])
        self.scales_loaded, self.qk_loaded, self.v_loaded, self.wo_loaded, self.ffn_loaded = (
            ctx.enter_context(nc.semaphore(n)) for n in (
                "w_scales_loaded", "w_qk_loaded", "w_v_loaded", "w_o_loaded", "w_ffn_loaded"))

    def load_scales(self, eng, layer):
        for i, t in enumerate(self.dram[1:3]):
            eng.dma_start(self.scales[:, i, :], t[bass.ds(layer, 1), :].broadcast_to([P, DH])).then_inc(self.scales_loaded, 16)

    def load_qkv(self, eng, layer, part):
        cols = slice(part * INNER, (part + 1) * INNER)
        src = self.dram[0][bass.ds(layer, 1), :, cols].rearrange("o d f -> (o d) f")
        eng.dma_start(self.qkv[:, cols], src).then_inc(self.v_loaded if part == 2 else self.qk_loaded, 16)

    def load_wo(self, eng, layer):
        wo = self.dram[3]
        eng.dma_start(self.wo[:], wo[bass.ds(layer, 1), :, :].rearrange("o (c p) m -> (o p) c m", p=P)).then_inc(self.wo_loaded, 16)

    def load_ffn(self, eng, layer):
        lg, lb, w1, b1, w2, b2 = self.dram[4:]
        one, loaded = bass.ds(layer, 1), self.ffn_loaded
        for dst, src in ((self.lg, lg), (self.lb, lb), (self.b2, b2)):
            eng.dma_start(dst[:], src[one, :].rearrange("o (p q) -> (o p) q", q=1)).then_inc(loaded, 16)
        eng.dma_start(self.w1[:], w1[one, :, :].rearrange("o d f -> (o d) f")).then_inc(loaded, 16)
        for part in range(2):
            for i, (off, sz) in enumerate(FCH):
                src = b1[one, part * F + off:part * F + off + sz].rearrange("o (p q) -> (o p) q", q=1)
                eng.dma_start(self.b1[0:sz, part, i:i + 1], src).then_inc(loaded, 16)
        for i, (off, sz) in enumerate(FCH):
            eng.dma_start(self.w2[0:sz, i, :], w2[one, off:off + sz, :].rearrange("o f m -> (o f) m")).then_inc(loaded, 16)


KINDS = ("q", "k", "v0", "v1", "qT", "kT", "S", "PT", "O", "OT", "W", "mean", "var", "h0", "h1", "h2", "y")
RING = 4


class Stretch:

    def __init__(self, tiles, groups, second, carry_in, carry_out):
        self.count, self.groups, self.carry_in = len(tiles), groups, carry_in
        self.made = range(int(carry_in), len(tiles) + int(carry_out))
        self.tiles = tiles + ([BATCH[1][0]] if carry_out else [])
        order = []
        if groups:
            order += [("mean", 0), ("mean", 1), ("qT", 0), ("kT", 0), ("var", 0), ("var", 1), ("S", 0), ("h0", 0), ("h1", 0), ("h2", 0),
                      ("h0", 1), ("y", 0), ("h1", 1), ("h2", 1), ("y", 1)]
            order += [("q", 1), ("k", 1), ("PT", 0), ("v0", 1), ("v1", 1), ("O", 0), ("qT", 1), ("kT", 1)]
        pair = [[("mean", 2), ("mean", 3)], [("var", 2)], [("h0", 2), ("h1", 2), ("h2", 2), ("y", 2)],
                [("var", 3)], [("h0", 3), ("h1", 3), ("h2", 3), ("y", 3)]]
        stages = [("q", 0), ("k", 0), ("v0", 1), ("PT", 2), ("v1", 1), ("O", 2), ("OT", 3), ("S", 1), ("qT", 0), ("kT", 0)]
        for i in range(self.count + 3):
            for kind, late in stages:
                there = i - late in (self.made if kind in ("q", "k", "v0", "v1") else range(self.count))
                if there and (kind, i - late) not in order:
                    order.append((kind, i - late))
            if i >= 3 and (i - 3) % TPG == TPG - 1:
                order.append(("W", (i - 3) // TPG))
            if groups and i >= second:
                order += sum(pair[i - second:i - second + 1] if i < self.count + 2 else pair[i - second:], [])
        self.order = order
        self.place = {unit: k for k, unit in enumerate(order)}
        self.hidden = [u for u in order if u[0][0] == "h"]


BATCH = [list(range(b * QT, (b + 1) * QT)) for b in range(B)]
FIRST = Stretch(BATCH[0], [], 0, False, True)
MIDDLE = Stretch(BATCH[1] + BATCH[0], [0, 1, 2, 3], QT + 3, True, True)
LAST = Stretch(BATCH[1], [0, 1, 2, 3], QT + 2, True, False)


def layers(nc, c, wt):
    with ExitStack() as ctx:
        sb = lambda n, s, d=F32: ctx.enter_context(nc.sbuf_tensor(n, s, d))
        ring = ctx.enter_context(nc.psum_tensor("ring", [P, RING, 2 * GT], F32))
        raw = sb("raw", [P, 2, INNER])
        sqr = sb("squares", [P, 2, INNER])
        rot = sb("rot", [P, 2, INNER])
        rot2 = sb("rot2", [P, 2, INNER])
        ss, yv, tv, uv = (sb(n, [P, 2 * HEADS]) for n in ("ss", "rsqrt", "newton1", "newton2"))
        rope = sb("rope_layer", [P, B, 2, 2, QT, DH])
        qT, kT = sb("qT", [P, NC, P]), sb("kT", [P, NC, 2, WIN + P])
        v = sb("v_win", [P, 2, WPT, NC, DH])
        prob = sb("l_prob", [P, NC, 2, 2 * WIN])
        nm, rs = sb("nmax_l", [P, 2, NC]), sb("rsum", [P, NC, 2])
        pT, o = sb("pT", [P, NC, P]), sb("o_win", [P, NC, 2, DH])
        oT = sb("oT_grp", [P, NC, GT])
        xn, sd = (sb(n, [P, 2, GT]) for n in ("f_xn", "f_sd"))
        gl, hh = sb("gelu", [P, 2, GT]), sb("hidden", [P, 4, GT])
        kT_cleared = ctx.enter_context(nc.semaphore("kT_cleared"))
        sems = []

        def sem(n):
            sems.append(ctx.enter_context(nc.semaphore(n)))
            return sems[-1]

        filled = {kind: sem(f"{kind}_filled_l") for kind in KINDS}
        drained = [sem(f"slot{s}_drained") for s in range(RING)]
        rope_ready = [sem(f"rope{b}_ready") for b in range(B)]
        sq_ready, t1_ready, t2_ready, rot_ready, unit_ready = (
            [sem(f"{n}_{x}_ready") for x in "qk"] for n in ("sq", "t1", "t2", "rot", "unit"))
        ss_ready, rsqrt_step, rsqrt_ready = sem("ss_ready"), sem("rsqrt_step"), sem("rsqrt_ready")
        nm_ready, exp_ready, rs_ready, rr_ready = (sem(n) for n in (
            "nm_ready", "exp_ready", "rsum_ready", "rrec_ready"))
        xsF_ready, fsq_ready, rsd_ready, norm_ready, xn_ready, gelu_ready, xsA_ready = (sem(n) for n in (
            "xsF_ready", "f_sq_ready", "f_rsd_ready", "f_norm_ready", "f_xn_ready", "gelu_ready", "xsA_ready"))
        assert sems[-1].num - sems[0].num == len(sems) - 1

        def by_rc(ap):
            return ap.rearrange("p (r c k) -> p r c k", r=2, c=NC)

        with nc.Block() as block:

            @block.gpsimd
            def _(pool):
                nc.gpsimd.memset(kT[:], 0.0).then_inc(kT_cleared, 1)
                pool.wait_ge(kT_cleared, 1)

        def run(st, layer, ropes, load):
            order, place, tiles, groups = st.order, st.place, st.tiles, st.groups
            n_tiles, made = st.count, st.made
            change = tiles.index(0) if 0 in tiles else None

            def slot(kind, n):
                return place[kind, n] % RING

            def read(kind, n):
                return drained[slot(kind, n)], place[kind, n] // RING + 1

            def unit(kind, n):
                return ring[:, slot(kind, n), :]

            with nc.Block() as block:

                if load:
                    @block.sync
                    def _(sp):
                        wt.load_scales(sp, layer + 1)
                        sp.wait_ge(filled["k"], QT)
                        wt.load_qkv(sp, layer + 1, 0)
                        wt.load_qkv(sp, layer + 1, 1)
                        sp.wait_ge(filled["v1"], QT)
                        wt.load_qkv(sp, layer + 1, 2)
                        sp.wait_ge(filled["W"], QT // TPG)
                        wt.load_wo(sp, layer + 1)
                        sp.wait_ge(*read("y", NG - 1))
                        wt.load_ffn(sp, layer + 1)

                @block.gpsimd
                def _(pool):
                    def tables(b):
                        pool.wait_ge(wt.scales_loaded, (layer + 2) * wt.SCALES)
                        for x in range(2):
                            nc.gpsimd.tensor_tensor(rope[:, b, x, 0, :, :], c.rope[:, :, 2 * x, :],
                                                    wt.scales[:, x, None, :].broadcast_to([P, QT, DH]), ALU.mult).then_inc(rope_ready[b], 1)
                            for half in range(2):
                                mine, other = slice(32 * half, 32 * half + 32), slice(32 - 32 * half, 64 - 32 * half)
                                nc.gpsimd.tensor_tensor(rope[:, b, x, 1, :, mine], c.rope[:, :, 2 * x + 1, mine],
                                                        wt.scales[:, x, None, other].broadcast_to([P, QT, DH // 2]), ALU.mult).then_inc(rope_ready[b], 1)

                    if st.carry_in:
                        pool.sem_inc(rot_ready[0], 1)
                        pool.sem_inc(rot_ready[1], 1)
                        pool.sem_inc(unit_ready[1], 1)
                    if 0 in ropes:
                        tables(ropes[0])
                    for t in made:
                        for x in range(2):
                            pool.wait_ge(t1_ready[x], t + 1)
                            pool.wait_ge(t2_ready[x], t + 1)
                            nc.gpsimd.tensor_tensor(rot[:, x, :], rot[:, x, :], rot2[:, x, :], ALU.add).then_inc(rot_ready[x], 1)
                        pool.wait_ge(rsqrt_ready, t + 1)
                        pool.wait_ge(rot_ready[1], t + 1)
                        kv = rot[:, 1, :].rearrange("p (h d) -> p h d", h=HEADS)
                        nc.gpsimd.tensor_tensor(kv, kv, yv[:, HEADS:, None].broadcast_to([P, HEADS, DH]),
                                                ALU.mult).then_inc(unit_ready[1], 1)
                        if t >= 1 and t in ropes:
                            tables(ropes[t])

                @block.scalar
                def _(act):
                    def evacuate(kind, n, out, in_=None):
                        act.wait_ge(filled[kind], n + 1)
                        nc.scalar.activation(out, unit(kind, n) if in_ is None else in_, ACT.Copy).then_inc(drained[slot(kind, n)], 1)

                    def square(x, n):
                        act.wait_ge(*read("qk"[x], n))
                        if n >= 1:
                            act.wait_ge(ss_ready, 2 * (n - 1) + x + 1)
                        nc.scalar.activation(sqr[:, x, :], raw[:, x, :], ACT.Square).then_inc(sq_ready[x], 1)

                    if st.carry_in:
                        act.sem_inc(sq_ready[0], 1)
                        act.sem_inc(sq_ready[1], 1)

                    def exponentials(n):
                        act.wait_ge(*read("S", n))
                        nc.scalar.activation(prob[:], prob[:], ACT.Exp, scale=8.0).then_inc(exp_ready, 1)

                    def late_exp(n):
                        return n + 1 < n_tiles and place["kT", n + 1] < place["PT", n]

                    for kind, n in order:
                        if kind in ("q", "k"):
                            x = "qk".index(kind)
                            if n >= 1:
                                act.wait_ge(t1_ready[x], n)
                                act.wait_ge(t2_ready[x], n)
                            evacuate(kind, n, raw[:, x, :])
                            if kind == "q" or not (n >= 2 and place[kind, n] < place["PT", n - 2]):
                                square(x, n)
                        elif kind in ("v0", "v1"):
                            j = 2 * int(kind[1])
                            if n >= 2:
                                act.wait_ge(filled["O"], n - 1)
                            evacuate(kind, n, v[:, n % 2, j:j + 2, :, :].rearrange("p j c d -> p (j c d)"))
                        elif kind == "S" and not late_exp(n):
                            exponentials(n)
                        elif kind == "qT":
                            if n >= 1:
                                act.wait_ge(filled["S"], n)
                            evacuate(kind, n, qT[:].rearrange("p c t -> p (c t)"))
                        elif kind == "kT":
                            src = unit(kind, n).rearrange("p (c t) -> p c t", c=NC)
                            if n >= 1:
                                act.wait_ge(filled["S"], n)
                            act.wait_ge(filled[kind], n + 1)
                            nc.scalar.activation(kT[:, :, n % 2, WIN:], src, ACT.Copy)
                            lead = src[:, :, P - WIN:] if (n + 1) % QT else c.xsA[:, None, 0:XPAD].broadcast_to([P, NC, WIN])
                            nc.scalar.activation(kT[:, :, (n + 1) % 2, 0:WIN], lead, ACT.Copy).then_inc(drained[slot(kind, n)], 1)
                            if n >= 1 and late_exp(n - 1):
                                exponentials(n - 1)
                        elif kind == "PT":
                            if n >= 1:
                                act.wait_ge(filled["O"], n)
                            evacuate(kind, n, pT[:].rearrange("p c t -> p (c t)"))
                            if n + 2 in made and place["k", n + 2] < place[kind, n]:
                                square(1, n + 2)
                        elif kind == "OT":
                            if n % TPG == 0 and n:
                                act.wait_ge(filled["W"], n // TPG)
                            evacuate(kind, n, oT[:, :, (n % TPG) * P:(n % TPG + 1) * P],
                                     unit(kind, n).rearrange("p (c t) -> p c t", c=NC))
                        elif kind == "mean":
                            act.wait_ge(*read(kind, n))
                            if n >= 2:
                                act.wait_ge(norm_ready, n - 1)
                            nc.scalar.activation(sd[:, n % 2, :], xn[:, n % 2, :], ACT.Square).then_inc(fsq_ready, 1)
                        elif kind == "var":
                            act.wait_ge(filled["var"], n + 1)
                            nc.scalar.activation(sd[:, n % 2, :], unit(kind, n)[:, 0:GT], ACT.Sqrt,
                                                 bias=c.eps[:, 0:1]).then_inc(drained[slot(kind, n)], 1)
                        elif kind[0] == "h":
                            ch, m = int(kind[1]), st.hidden.index((kind, n))
                            sz = FCH[ch][1]
                            act.wait_ge(filled[kind], n + 1)
                            if m == 0:
                                act.wait_ge(wt.ffn_loaded, (layer + 1) * wt.FFN)
                            if m >= 2:
                                act.wait_ge(*read(*st.hidden[m - 2]))
                            nc.scalar.activation(gl[0:sz, m % 2, :], unit(kind, n)[0:sz, 0:GT], ACT.Gelu,
                                                 bias=wt.b1[0:sz, 1, ch:ch + 1]).then_inc(gelu_ready, 1)

                @block.vector
                def _(dve):
                    steps = [0]

                    def step(ins):
                        steps[0] += 1
                        ins.then_inc(rsqrt_step, 1)
                        dve.wait_ge(rsqrt_step, steps[0])

                    def rotate(t, x):
                        def heads(ap):
                            return ap.rearrange("p (h e d) -> p h e d", h=HEADS, e=2)

                        def table(i):
                            return rope[:, tiles[t] // QT, x, i, tiles[t] % QT, :].rearrange(
                                "p (o e d) -> p o e d", o=1, e=2).broadcast_to([P, HEADS, 2, DH // 2])

                        dve.wait_ge(*read("qk"[x], t))
                        if t == change and x == 0:
                            dve.wait_ge(rope_ready[0], 6)
                        if t == n_tiles and x == 0:
                            dve.wait_ge(rope_ready[1], 6)
                        if t >= 1:
                            dve.wait_ge(filled["qT" if x == 0 else "kT"], t)
                            dve.wait_ge(rot_ready[x], t)
                        nc.vector.tensor_tensor(heads(rot[:, x, :]), heads(raw[:, x, :]), table(0), ALU.mult).then_inc(t1_ready[x], 1)
                        nc.vector.tensor_tensor(heads(rot2[:, x, :]), heads(raw[:, x, :])[:, :, ::-1, :], table(1), ALU.mult).then_inc(t2_ready[x], 1)

                    def lengths(t):
                        for x in range(2):
                            dve.wait_ge(sq_ready[x], t + 1)
                            nc.vector.tensor_reduce(ss[:, x * HEADS:(x + 1) * HEADS], sqr[:, x, :].rearrange("p (h d) -> p h d", h=HEADS),
                                                    AX.X, ALU.add).then_inc(ss_ready, 1)
                        dve.wait_ge(ss_ready, 2 * t + 2)
                        if t >= 1:
                            dve.wait_ge(unit_ready[0], t)
                            dve.wait_ge(unit_ready[1], t)
                        step(nc.vector.tensor_scalar(ss[:], ss[:], 1e-24, None, ALU.max))
                        step(nc.vector.tensor_scalar(yv[:].bitcast(I32), ss[:].bitcast(I32), 1, None, ALU.logical_shift_right))
                        step(nc.vector.tensor_scalar(yv[:].bitcast(I32), yv[:].bitcast(I32), -1.0, float(RSQRT_MAGIC), ALU.mult, ALU.add))
                        for it in range(3):
                            step(nc.vector.tensor_tensor(tv[:], ss[:], yv[:], ALU.mult))
                            step(nc.vector.scalar_tensor_tensor(uv[:], tv[:], -0.5, yv[:], ALU.mult, ALU.mult))
                            last = nc.vector.scalar_tensor_tensor(yv[:], uv[:], 1.5, yv[:], ALU.add, ALU.mult)
                            if it < 2:
                                step(last)
                        last.then_inc(rsqrt_ready, 1)

                    def unit_q(t):
                        dve.wait_ge(rot_ready[0], t + 1)
                        dve.wait_ge(rsqrt_ready, t + 1)
                        qv = rot[:, 0, :].rearrange("p (h d) -> p h d", h=HEADS)
                        nc.vector.tensor_tensor(qv, qv, yv[:, 0:HEADS, None].broadcast_to([P, HEADS, DH]), ALU.mult).then_inc(unit_ready[0], 1)

                    def soft(n):
                        dve.wait_ge(filled["S"], n + 1)
                        nc.vector.tensor_reduce(nm[:], by_rc(unit("S", n)), AX.X, ALU.max, negate=True).then_inc(nm_ready, 1)
                        dve.wait_ge(nm_ready, n + 1)
                        if n >= 1:
                            dve.wait_ge(filled["PT"], n)
                        nc.vector.tensor_tensor(prob[:].rearrange("p c r k -> p r c k"), by_rc(unit("S", n)),
                                                nm[:, :, :, None].broadcast_to([P, 2, NC, 2 * WIN]), ALU.add).then_inc(drained[slot("S", n)], 1)

                    def sums(n):
                        dve.wait_ge(exp_ready, n + 1)
                        if n >= 1:
                            dve.wait_ge(*read("O", n - 1))
                        nc.vector.tensor_reduce(rs[:], prob[:], AX.X, ALU.add).then_inc(rs_ready, 1)
                        dve.wait_ge(rs_ready, n + 1)
                        nc.vector.reciprocal(rs[:], rs[:]).then_inc(rr_ready, 1)

                    def normalise(n):
                        dve.wait_ge(rr_ready, n + 1)
                        dve.wait_ge(filled["O"], n + 1)
                        if n >= 1:
                            dve.wait_ge(filled["OT"], n)
                        nc.vector.tensor_tensor(o[:], by_rc(unit("O", n)).rearrange("p r c d -> p c r d"),
                                                rs[:, :, :, None].broadcast_to([P, NC, 2, DH]), ALU.mult).then_inc(drained[slot("O", n)], 1)

                    if st.carry_in:
                        for x in range(2):
                            dve.sem_inc(t1_ready[x], 1)
                            dve.sem_inc(t2_ready[x], 1)
                        dve.sem_inc(ss_ready, 2)
                        dve.sem_inc(rsqrt_ready, 1)
                        dve.sem_inc(unit_ready[0], 1)

                    for kind, n in order:
                        s = drained[slot(kind, n)]
                        if kind == "k":
                            rotate(n, 0)
                            rotate(n, 1)
                            lengths(n)
                            unit_q(n)
                        elif kind == "S":
                            soft(n)
                            sums(n)
                        elif kind == "O":
                            normalise(n)
                        elif kind == "W":
                            group = tiles[n * TPG] // TPG
                            g = slice(group * GT, (group + 1) * GT)
                            dve.wait_ge(filled[kind], n + 1)
                            nc.vector.tensor_tensor(c.xT[:, g], unit(kind, n)[:, 0:GT], c.xT[:, g], ALU.add).then_inc(s, 1)
                            dve.wait_ge(*read(kind, n))
                            shift_copy(nc, c.xT, c.xsF, group).then_inc(xsF_ready, 1)
                        elif kind == "mean":
                            col = xcol(groups[n] * GT)
                            dve.wait_ge(filled[kind], n + 1)
                            if n >= 2:
                                dve.wait_ge(filled["h2"], n - 1)
                            nc.vector.tensor_tensor(xn[:, n % 2, :], c.xsF[:, col:col + GT], unit(kind, n)[:, 0:GT], ALU.subtract).then_inc(s, 1)
                        elif kind == "var":
                            dve.wait_ge(*read(kind, n))
                            nc.vector.reciprocal(sd[:, n % 2, :], sd[:, n % 2, :]).then_inc(rsd_ready, 1)
                            dve.wait_ge(rsd_ready, n + 1)
                            nc.vector.tensor_tensor(xn[:, n % 2, :], xn[:, n % 2, :], sd[:, n % 2, :], ALU.mult).then_inc(norm_ready, 1)
                            dve.wait_ge(norm_ready, n + 1)
                            if n == 0:
                                dve.wait_ge(wt.ffn_loaded, (layer + 1) * wt.FFN)
                            nc.vector.tensor_scalar(xn[:, n % 2, :], xn[:, n % 2, :], wt.lg[:, 0:1], wt.lb[:, 0:1], ALU.mult, ALU.add).then_inc(xn_ready, 1)
                        elif kind[0] == "h":
                            ch, m = int(kind[1]), st.hidden.index((kind, n))
                            sz = FCH[ch][1]
                            dve.wait_ge(gelu_ready, m + 1)
                            if m >= 4:
                                dve.wait_ge(filled["y"], st.hidden[m - 4][1] + 1)
                            nc.vector.scalar_tensor_tensor(hh[0:sz, m % 4, :], unit(kind, n)[0:sz, GT:], wt.b1[0:sz, 0, ch:ch + 1],
                                                           gl[0:sz, m % 2, :], ALU.add, ALU.mult).then_inc(s, 1)
                        elif kind == "y":
                            g = slice(groups[n] * GT, (groups[n] + 1) * GT)
                            dve.wait_ge(filled[kind], n + 1)
                            nc.vector.scalar_tensor_tensor(c.xT[:, g], unit(kind, n)[:, 0:GT], wt.b2[:, 0:1], c.xT[:, g],
                                                           ALU.add, ALU.add).then_inc(s, 1)
                            dve.wait_ge(*read(kind, n))
                            shift_copy(nc, c.xT, c.xsA, groups[n]).then_inc(xsA_ready, 1)
                    if groups:
                        dve.wait_ge(xsA_ready, NG)

                @block.tensor
                def _(pe):
                    if st.carry_in:
                        for kind in ("q", "k", "v0", "v1"):
                            pe.sem_inc(filled[kind], 1)
                    for kind, n in order:
                        u = place[kind, n]
                        if u >= RING:
                            pe.wait_ge(drained[u % RING], u // RING)
                        ps = unit(kind, n)
                        if kind in ("q", "k"):
                            if kind == "q" and n == n_tiles and groups:
                                pe.wait_ge(xsA_ready, 3)
                            if kind == "q" and n == change:
                                pe.wait_ge(wt.qk_loaded, (layer + 2) * wt.QK)
                                if n >= 1:
                                    pe.wait_ge(xsA_ready, NG // 2)
                            x = "qk".index(kind)
                            col = xcol(tiles[n] * P)
                            for h in range(2):
                                f = x * INNER + h * GT
                                m = nc.tensor.matmul(ps[:, h * GT:(h + 1) * GT], c.xsA[:, col:col + P], wt.qkv[:, f:f + GT], start=True, stop=True)
                        elif kind in ("v0", "v1"):
                            if kind == "v0" and n == change:
                                pe.wait_ge(wt.v_loaded, (layer + 2) * wt.V)
                            wv = wt.qkv[:, 2 * INNER:].rearrange("p (c r d) -> p r c d", r=2, c=NC)
                            for jj in range(2):
                                col = xcol(tiles[n] * P) + (2 * int(kind[1]) + jj) * WIN - WIN
                                for r in range(2):
                                    m = nc.tensor.matmul(ps[64 * r:64 * r + 64, jj * GT:(jj + 1) * GT], c.xsA[:, col:col + 2 * WIN],
                                                         wv[:, r, :, :], start=True, stop=True)
                        elif kind in ("qT", "kT"):
                            x = "qk".index(kind[0])
                            pe.wait_ge(unit_ready[x], n + 1)
                            for ch in range(NC):
                                m = nc.tensor.transpose(ps[:, ch * P:(ch + 1) * P], rot[:, x, ch * P:(ch + 1) * P], c.ident[:])
                        elif kind == "S":
                            pe.wait_ge(*read("qT", n))
                            pe.wait_ge(*read("kT", n))
                            first_tile = int(n % QT == 0)
                            for r in range(2):
                                nc.tensor.matmul(ps[:, r * GT:(r + 1) * GT], c.identb[:],
                                                 c.mask[:, first_tile, None, :].broadcast_to([P, NC, 2 * WIN]),
                                                 start=True, stop=False, skip_group_check=True)
                            for ch in range(NC):
                                for r in range(2):
                                    for j in range(WPT):
                                        m = nc.tensor.matmul(
                                            ps[32 * j:32 * j + 32, r * GT + ch * 64:r * GT + ch * 64 + 64],
                                            qT[64 * r:64 * r + 64, ch, 32 * j:32 * j + 32],
                                            kT[64 * r:64 * r + 64, ch, n % 2, 32 * j:32 * j + 64],
                                            start=False, stop=(ch == NC - 1), skip_group_check=True)
                        elif kind == "PT":
                            pe.wait_ge(exp_ready, n + 1)
                            for ch in range(NC):
                                m = nc.tensor.transpose(ps[:, ch * P:(ch + 1) * P], prob[:, ch, :, :].rearrange("p r k -> p (r k)"), c.ident[:])
                        elif kind == "O":
                            for part in ("PT", "v0", "v1"):
                                if (part, n) in place:
                                    pe.wait_ge(*read(part, n))
                            for ch in range(NC):
                                for r in range(2):
                                    for j in range(WPT):
                                        m = nc.tensor.matmul(
                                            ps[32 * j:32 * j + 32, r * GT + ch * 64:r * GT + ch * 64 + 64],
                                            pT[64 * r:64 * r + 64, ch, 32 * j:32 * j + 32],
                                            v[64 * r:64 * r + 64, n % 2, j, ch, :], start=True, stop=True)
                        elif kind == "OT":
                            pe.wait_ge(*read("O", n))
                            for ch in range(NC):
                                m = nc.tensor.transpose(ps[:, ch * P:(ch + 1) * P], o[:, ch, :, :].rearrange("p r d -> p (r d)"), c.ident[:])
                        elif kind == "W":
                            pe.wait_ge(*read("OT", n * TPG + TPG - 1))
                            if change is not None and n * TPG == change:
                                pe.wait_ge(wt.wo_loaded, (layer + 2) * wt.WO)
                            for ch in range(NC):
                                m = nc.tensor.matmul(ps[:, 0:GT], wt.wo[:, ch, :], oT[:, ch, :], start=(ch == 0), stop=(ch == NC - 1))
                        elif kind == "mean":
                            if n >= 2:
                                pe.wait_ge(xsF_ready, n - 1)
                            col = xcol(groups[n] * GT)
                            m = nc.tensor.matmul(ps[:, 0:GT], c.ones_d[:], c.xsF[:, col:col + GT], start=True, stop=True)
                        elif kind == "var":
                            pe.wait_ge(fsq_ready, n + 1)
                            m = nc.tensor.matmul(ps[:, 0:GT], c.ones_d[:], sd[:, n % 2, :], start=True, stop=True)
                        elif kind[0] == "h":
                            off, sz = FCH[int(kind[1])]
                            pe.wait_ge(xn_ready, n + 1)
                            nc.tensor.matmul(ps[0:sz, 0:GT], wt.w1[:, F + off:F + off + sz], xn[:, n % 2, :], start=True, stop=True)
                            m = nc.tensor.matmul(ps[0:sz, GT:], wt.w1[:, off:off + sz], xn[:, n % 2, :], start=True, stop=True)
                        elif kind == "y":
                            for ch, (off, sz) in enumerate(FCH):
                                pe.wait_ge(*read(f"h{ch}", n))
                                m = nc.tensor.matmul(ps[:, 0:GT], wt.w2[0:sz, ch, :], hh[0:sz, st.hidden.index((f"h{ch}", n)) % 4, :],
                                                     start=(ch == 0), stop=(ch == len(FCH) - 1))
                        m.then_inc(filled[kind], 1)

            nc.all_engine_barrier()
            nc.gpsimd.sem_clear(range(sems[0].num, sems[-1].num + 1))
            nc.all_engine_barrier()

        run(FIRST, -1, {0: 0, 4: 1}, False)
        with nc.Fori(0, DEPTH - 1) as layer:
            run(MIDDLE, layer, {3: 0, 11: 1}, True)
        run(LAST, DEPTH - 1, {}, False)


def finish(nc, c, out):
    with ExitStack() as ctx:
        sb = lambda n, s, d=F32: ctx.enter_context(nc.sbuf_tensor(n, s, d))
        sem = lambda n: ctx.enter_context(nc.semaphore(n))
        ps = ctx.enter_context(nc.psum_tensor("fin_ps", [P, 8, GT], F32))
        xc, sq, sd, y, z, rows = (sb(n, [P, T]) for n in ("e_xc", "e_sq", "e_sd", "e_y", "e_z", "e_rows"))
        mean, xcr, sqr, var, sdr, rs, done = (sem(f"e_{n}") for n in ("mean", "xc", "sq", "var", "sd", "rs", "ln"))
        x_there, z_ready, zT_filled, rows_ready, stored = (sem(n) for n in ("x_there", "z_ready", "zT_filled", "rows_ready", "out_stored"))
        with nc.Block() as block:

            @block.sync
            def _(sp):
                for g in range(NG):
                    sp.wait_ge(rows_ready, g + 1)
                    sp.dma_start(out[g // 2, (g % 2) * GT:(g % 2 + 1) * GT, :].rearrange("(t p) d -> p t d", p=P),
                                 rows[:, g * GT:(g + 1) * GT].rearrange("p (t d) -> p t d", t=TPG)).then_inc(stored, 16)
                sp.wait_ge(stored, 16 * NG)

            @block.tensor
            def _(pe):
                pe.sem_inc(x_there, NG)
                layer_norm_pe(nc, pe, c.ones_d, grp(c.xT), grp(sq), lambda g: ps[:, g, :], lambda g: ps[:, 4 + g, :],
                              x_there, sqr, mean, var)
                for g in range(NG):
                    pe.wait_ge(z_ready, g + 1)
                    for j in range(TPG):
                        t = g * TPG + j
                        m = nc.tensor.transpose(ps[:, g, j * P:(j + 1) * P], z[:, t * P:(t + 1) * P], c.ident[:])
                    m.then_inc(zT_filled, 1)

            @block.scalar
            def _(act):
                layer_norm_act(nc, act, c.eps, grp(xc), grp(sq), lambda g: ps[:, 4 + g, :], grp(sd), xcr, sqr, var, sdr)
                for g in range(NG):
                    act.wait_ge(zT_filled, g + 1)
                    nc.scalar.activation(grp(rows)(g), ps[:, g, :], ACT.Copy).then_inc(rows_ready, 1)

            @block.vector
            def _(dve):
                layer_norm_dve(nc, dve, grp(c.xT), grp(xc), lambda g: ps[:, g, :], grp(sd), grp(y), mean, xcr, sdr, rs, done)
                for g in range(NG):
                    dve.wait_ge(done, g + 1)
                    nc.vector.tensor_tensor(grp(z)(g), grp(c.x1)(g), grp(y)(g), ALU.add).then_inc(z_ready, 1)


class Chip:

    def __init__(self, nc, ctx, ident, rope, mask):
        sb = lambda n, s, d=F32: ctx.enter_context(nc.sbuf_tensor(n, s, d))
        self.ident_dram, self.rope_dram, self.mask_dram = ident, rope, mask
        self.ident, self.identb = sb("ident", [P, P]), sb("identb", [P, P], BF16)
        self.ones_d, self.eps = sb("ones_d", [P, P]), sb("eps", [P, 1])
        self.mask32, self.mask = sb("mask32", [P, 2, 2 * WIN]), sb("mask", [P, 2, 2 * WIN], BF16)
        self.rope = sb("rope", [P, QT, 4, DH])
        self.x0, self.xT = sb("x0", [P, T]), sb("xT", [P, T])
        self.x1 = self.x0
        self.xsA, self.xsF = sb("xsA", [P, B * XB]), sb("xsF", [P, B * XB])


def program(nc, x, wqkv1, wproj, bproj, wqkv, qs, ks, wo, lg, lb, w1, b1, w2, b2, ident, rope, mask, out):
    with ExitStack() as ctx:
        c = Chip(nc, ctx, ident, rope, mask)
        wt = Weights(nc, ctx, wqkv, qs, ks, wo, lg, lb, w1, b1, w2, b2)
        with nc.sbuf_tensor("o_tok", [P, NT, D], F32) as c.o_tok:
            load_and_project(nc, c, x, wqkv1, wt)
            project(nc, c, wproj, bproj)
        layers(nc, c, wt)
        finish(nc, c, out)


def constants():
    import numpy as np
    f = np.float32
    half = np.arange(0, DH, 2, dtype=f)
    inv = (f(1.0) / np.power(f(10000.0), half / f(DH))).astype(f)
    t = np.arange(N, dtype=f)
    ang = (t[:, None] * inv[None, :]).astype(f)
    base = ((half + f(0.4 * DH)) / f(1.4 * DH)).astype(f)
    power = ((t - f(N // 2)) / f(WIN // 2)).astype(f)
    scale = np.power(base[None, :], power[:, None]).astype(f)
    cos, sin = np.cos(ang).astype(f), np.sin(ang).astype(f)
    rec = (f(1.0) / scale).astype(f)
    tab = np.stack([np.concatenate([a, b], -1) for a, b in (
        (cos * scale, cos * scale), (-sin * scale, sin * scale), (cos * rec, cos * rec), (-sin * rec, sin * rec))], 1)
    tab = np.ascontiguousarray(tab.reshape(QT, P, 4, DH).transpose(1, 0, 2, 3)).astype(f)
    i, j = np.arange(P)[:, None] % WIN, np.arange(2 * WIN)[None, :] - WIN
    ordinary = np.where((j > i) | (i > j + WIN), f(NEG), f(0))
    start = np.where((np.arange(P)[:, None] < WIN) & (j < 0), f(NEG), ordinary)
    return np.eye(P, dtype=f), tab, np.ascontiguousarray(np.stack([ordinary, start], 1)).astype(f)


_INS = ["L0_attn_x", "L0_attn_Wqkv", "L0_attn_Wproj", "L0_attn_bproj", "L0_ffn_Wqkv", "L0_ffn_q_scale", "L0_ffn_k_scale",
        "L0_ffn_Wo", "L0_ffn_ln_g", "L0_ffn_ln_b", "L0_ffn_W1", "L0_ffn_b1", "L0_ffn_W2", "L0_ffn_b2"]


def kernel(**inputs):
    import numpy as _np
    import concourse.bacc as _bacc
    from concourse import mybir as _mybir
    from concourse.bass_utils import run_bass_kernel_spmd as _run

    nc = _bacc.Bacc("TRN2", target_bir_lowering=False, num_devices=1)
    arrays, args = {}, []
    ident, rope, mask = constants()
    for name, a in [(n, inputs[n]) for n in _INS] + [("ident", ident), ("rope", rope), ("mask", mask)]:
        a = _np.ascontiguousarray(a)
        arrays[f"in_{name}"] = a
        args.append(nc.dram_tensor(f"in_{name}", a.shape, _mybir.dt.from_np(a.dtype), kind="ExternalInput").ap())
    args.append(nc.dram_tensor("out", (B, N, D), _mybir.dt.float32, kind="ExternalOutput").ap())
    program(nc, *args)
    r = _run(nc, [arrays], core_ids=[0])
    return r.results[0]["out"]
```
